# Optimizing a Trainium2 kernel written in Bass

```python
import numpy as np
import jax
import jax.numpy as jnp

def _softmax(x, axis=-1):
    return jax.nn.softmax(x, axis=axis)

def _gelu(x):
    return jax.nn.gelu(x, approximate=True)

def _silu(x):
    return jax.nn.silu(x)

def _sigmoid(x):
    return jax.nn.sigmoid(x)

def _layernorm(x, axis=-1, eps=1e-05):
    m = jnp.mean(x, axis=axis, keepdims=True)
    v = jnp.var(x, axis=axis, keepdims=True)
    return (x - m) / jnp.sqrt(v + eps)

def _scatter_add(tgt, idx, src, axis=0):
    return tgt.at[idx].add(src)

def _segment_sum(src, seg, n):
    return jax.ops.segment_sum(src, seg, n)
kernel_name = 'mk_seq_postln_d1_jaxref_r4_5794e5'

def setup_inputs(seed: int=0):
    np.random.seed(seed)
    _w = jnp.asarray

    def _L0_attn_setup():
        import jax, jax.numpy as jnp
        import numpy as np
        B, S, E = (4, 512, 256)
        H = 16
        D = E // H
        WIN = 128

        def _sliding_window_attention(q, k, v, win):
            b, h, s, d = q.shape
            nb = s // win
            scale = 1.0 / jnp.sqrt(jnp.float32(d))
            qb = q.reshape(b, h, nb, win, d)
            kb = k.reshape(b, h, nb, win, d)
            vb = v.reshape(b, h, nb, win, d)
            zpad = jnp.zeros_like(kb[:, :, :1])
            k2 = jnp.concatenate([jnp.concatenate([zpad, kb[:, :, :-1]], axis=2), kb], axis=3)
            v2 = jnp.concatenate([jnp.concatenate([zpad, vb[:, :, :-1]], axis=2), vb], axis=3)
            scores = jnp.einsum('bhnqd,bhnkd->bhnqk', qb, k2) * scale
            qi = jnp.arange(win)[:, None]
            kj = jnp.arange(2 * win)[None, :]
            delta = qi - kj + win
            valid = (delta >= 0) & (delta <= win)
            blk = jnp.arange(nb)[:, None, None]
            valid = valid[None] & (blk * win + (kj[None] - win) >= 0)
            slopes = jnp.exp2(-(jnp.arange(H, dtype=jnp.float32) + 1.0) * 8.0 / H)
            bias = slopes[:, None, None] * delta.astype(jnp.float32)
            scores = jnp.where(valid[None, :, :, :, :][:, None].squeeze(0)[None] if False else valid[None, None], scores + bias[None, :, None], -jnp.inf)
            p = jax.nn.softmax(scores, axis=-1)
            out = jnp.einsum('bhnqk,bhnkd->bhnqd', p, v2)
            return out.reshape(b, h, s, d)
        key = jax.random.key(seed)
        k1, k2, k3 = jax.random.split(key, 3)
        x = jax.random.normal(k1, (B, S, E), dtype=jnp.float32)
        w_in = jax.random.normal(k2, (3 * E, E), dtype=jnp.float32) * 0.02
        w_out = jax.random.normal(k3, (E, E), dtype=jnp.float32) * 0.02
        return {'x': x, 'w_in': w_in, 'w_out': w_out}
    _L0_attn_in = _L0_attn_setup()

    def _L0_ffn_setup():
        import jax, jax.numpy as jnp
        import numpy as np
        from jax import lax
        T, B, I, M, O = (64, 64, 256, 256, 256)

        def _xavier(key, shape):
            fan_out, fan_in = shape
            limit = float(np.sqrt(6.0 / (fan_in + fan_out)))
            return jax.random.uniform(key, shape, jnp.float32, -limit, limit)
        key = jax.random.key(seed)
        ks = jax.random.split(key, 9)
        x = jax.random.normal(ks[0], (T, B, I), jnp.float32)
        return {'x': x, 'wf': _xavier(ks[1], (M, I)), 'uf': _xavier(ks[2], (M, M)), 'bf': jnp.zeros((M,), jnp.float32), 'wi': _xavier(ks[3], (M, I)), 'ui': _xavier(ks[4], (M, M)), 'bi': jnp.zeros((M,), jnp.float32), 'wc': _xavier(ks[5], (M, I)), 'uc': _xavier(ks[6], (M, M)), 'bc': jnp.zeros((M,), jnp.float32), 'wo': _xavier(ks[7], (O, I)), 'uo': _xavier(ks[8], (O, M)), 'bo': jnp.zeros((O,), jnp.float32), 'in_c': jnp.zeros((M,), jnp.float32)}
    _L0_ffn_in = _L0_ffn_setup()
    _d = {'L0_attn_x': _L0_attn_in['x'], 'L0_attn_w_in': _L0_attn_in['w_in'], 'L0_attn_w_out': _L0_attn_in['w_out'], 'L0_ffn_wf': _L0_ffn_in['wf'], 'L0_ffn_uf': _L0_ffn_in['uf'], 'L0_ffn_bf': _L0_ffn_in['bf'], 'L0_ffn_wi': _L0_ffn_in['wi'], 'L0_ffn_ui': _L0_ffn_in['ui'], 'L0_ffn_bi': _L0_ffn_in['bi'], 'L0_ffn_wc': _L0_ffn_in['wc'], 'L0_ffn_uc': _L0_ffn_in['uc'], 'L0_ffn_bc': _L0_ffn_in['bc'], 'L0_ffn_wo': _L0_ffn_in['wo'], 'L0_ffn_uo': _L0_ffn_in['uo'], 'L0_ffn_bo': _L0_ffn_in['bo'], 'L0_ffn_in_c': _L0_ffn_in['in_c']}
    _x0 = _d['L0_attn_x']
    _d['L0_attn_x'] = jax.random.normal(jax.random.fold_in(jax.random.key(seed), 1), (16, 512, 256), dtype=_x0.dtype)
    del _x0
    return _d

def reference(L0_attn_x, L0_attn_w_in, L0_attn_w_out, L0_ffn_wf, L0_ffn_uf, L0_ffn_bf, L0_ffn_wi, L0_ffn_ui, L0_ffn_bi, L0_ffn_wc, L0_ffn_uc, L0_ffn_bc, L0_ffn_wo, L0_ffn_uo, L0_ffn_bo, L0_ffn_in_c):

    def _L0_attn_ref(x, w_in, w_out):
        import jax, jax.numpy as jnp
        import numpy as np
        B, S, E = (4, 512, 256)
        H = 16
        D = E // H
        WIN = 128

        def _sliding_window_attention(q, k, v, win):
            b, h, s, d = q.shape
            nb = s // win
            scale = 1.0 / jnp.sqrt(jnp.float32(d))
            qb = q.reshape(b, h, nb, win, d)
            kb = k.reshape(b, h, nb, win, d)
            vb = v.reshape(b, h, nb, win, d)
            zpad = jnp.zeros_like(kb[:, :, :1])
            k2 = jnp.concatenate([jnp.concatenate([zpad, kb[:, :, :-1]], axis=2), kb], axis=3)
            v2 = jnp.concatenate([jnp.concatenate([zpad, vb[:, :, :-1]], axis=2), vb], axis=3)
            scores = jnp.einsum('bhnqd,bhnkd->bhnqk', qb, k2) * scale
            qi = jnp.arange(win)[:, None]
            kj = jnp.arange(2 * win)[None, :]
            delta = qi - kj + win
            valid = (delta >= 0) & (delta <= win)
            blk = jnp.arange(nb)[:, None, None]
            valid = valid[None] & (blk * win + (kj[None] - win) >= 0)
            slopes = jnp.exp2(-(jnp.arange(H, dtype=jnp.float32) + 1.0) * 8.0 / H)
            bias = slopes[:, None, None] * delta.astype(jnp.float32)
            scores = jnp.where(valid[None, :, :, :, :][:, None].squeeze(0)[None] if False else valid[None, None], scores + bias[None, :, None], -jnp.inf)
            p = jax.nn.softmax(scores, axis=-1)
            out = jnp.einsum('bhnqk,bhnkd->bhnqd', p, v2)
            return out.reshape(b, h, s, d)
        b, s, e = x.shape
        qkv = jnp.einsum('bse,fe->bsf', x, w_in)
        q, k, v = jnp.split(qkv, 3, axis=-1)

        def heads(t):
            return t.reshape(b, s, H, D).transpose(0, 2, 1, 3)
        o = _sliding_window_attention(heads(q), heads(k), heads(v), WIN)
        o = o.transpose(0, 2, 1, 3).reshape(b, s, e)
        return jnp.einsum('bse,fe->bsf', o, w_out)

    def _L0_ffn_ref(x, wf, uf, bf, wi, ui, bi, wc, uc, bc, wo, uo, bo, in_c):
        import jax, jax.numpy as jnp
        import numpy as np
        from jax import lax
        T, B, I, M, O = (64, 64, 256, 256, 256)

        def _xavier(key, shape):
            fan_out, fan_in = shape
            limit = float(np.sqrt(6.0 / (fan_in + fan_out)))
            return jax.random.uniform(key, shape, jnp.float32, -limit, limit)
        batch = x.shape[1]
        c0 = jnp.broadcast_to(in_c, (batch, in_c.shape[0]))

        def step(c, xt):
            ft = jax.nn.sigmoid(xt @ wf.T + c @ uf.T + bf)
            it = jax.nn.sigmoid(xt @ wi.T + c @ ui.T + bi)
            gt = jnp.tanh(xt @ wc.T + c @ uc.T + bc)
            c = ft * c + it * gt
            return (c, None)
        c_final, _ = lax.scan(step, c0, x)
        h = jnp.tanh(jnp.einsum('tbi,oi->tbo', x, wo) + c_final @ uo.T + bo)
        return h
    x = L0_attn_x
    x = _layernorm(x + _L0_attn_ref(x, L0_attn_w_in, L0_attn_w_out), axis=-1)
    x = _layernorm(x + _L0_ffn_ref(x, L0_ffn_wf, L0_ffn_uf, L0_ffn_bf, L0_ffn_wi, L0_ffn_ui, L0_ffn_bi, L0_ffn_wc, L0_ffn_uc, L0_ffn_bc, L0_ffn_wo, L0_ffn_uo, L0_ffn_bo, L0_ffn_in_c), axis=-1)
    return x

_drawn_inputs = setup_inputs


def setup_inputs(seed=0):
    import zlib

    import numpy as np

    out = dict(_drawn_inputs(seed))
    spreads = {'L0_ffn_bf': (0.0, 0.731),
     'L0_ffn_bi': (0.0, 0.691),
     'L0_ffn_bc': (0.0, 0.1),
     'L0_ffn_bo': (0.0, 0.1),
     'L0_ffn_in_c': (0.0, 0.8)}
    factors = {}
    for name, (base, spread) in spreads.items():
        noise = np.random.default_rng([zlib.crc32(name.encode()), seed]).standard_normal(out[name].shape)
        drawn = base * np.exp(spread * noise) if base else spread * noise
        out[name] = jnp.asarray(drawn.astype(out[name].dtype))
    for name, factor in factors.items():
        out[name] = (out[name] * factor).astype(out[name].dtype)
    return out
```

```python
import numpy as np
import concourse.bass as bass
from concourse import mybir
from contextlib import ExitStack

B, S, E = 16, 512, 256
H = 16
D = E // H
WIN = 128
NB = S // WIN
KC = E // 128
QUADS = H // 4
EPS = 1e-5
MASKED = -1e30

ROWS_Q = ((0, 0, 2), (2 * D, 0, 1))
ROWS_K = ((0, 0, 1), (D, 0, 2))
ROW_TILE = 3 * D
N_TILES = 8
ROW_BIAS = ROW_TILE + N_TILES
ROW_MAX = ROW_BIAS + 2
K_MAXIMA = ROW_MAX
K_SCORES = ROW_MAX + 1
PITCH = D + 1
VCOLS = H * PITCH + 16

STACK_DMAS = 8
MAXROW_DMAS = 2


def build(nc, x, xt, w_in, w_out, w_gates, u_gates, b_gates, w_o, u_o, b_o, in_c, pos_bias, tile_rows, out):
    F32, F32R, BF16 = mybir.dt.float32, mybir.dt.float32r, mybir.dt.bfloat16
    ACT, ALU, AX = mybir.ActivationFunctionType, mybir.AluOpType, mybir.AxisListType
    ctx = ExitStack()
    with ctx:
        def sb(name, shape, dt=F32):
            return ctx.enter_context(nc.sbuf_tensor(name, shape, dt))

        def sem(name):
            return ctx.enter_context(nc.semaphore(name))

        Win = sb("Win", [128, 2, KC, 3 * E], F32R)
        Wout = sb("Wout", [128, 2, KC, E], F32R)
        Wg = sb("Wg", [128, 2, KC, 3 * E], F32R)
        Ug = sb("Ug", [128, 2, KC, 3 * E], F32R)
        Wo = sb("Wo", [128, 2, KC, E], F32R)
        Uo = sb("Uo", [128, 2, KC, E], F32R)
        Qs = sb("Qs", [128, H // 2, S], F32R)
        Ks = sb("Ks", [128, H // 2, S], F32R)
        qk_parts = sb("qk_parts", [128, 2, 2, 2, S], F32R)
        Vp = sb("Vp", [128, NB, VCOLS])
        Pt = sb("Pt", [128, 4, 2 * S])
        xt_raw = sb("xt_raw", [128, KC, S])
        xT = sb("xT", [128, 2, KC, S], F32R)
        max_q = sb("max_q", [128, 16])
        max_rows = sb("max_rows", [16, 128], F32R)
        ctx_raw = sb("ctx_raw", [128, S])
        rden = sb("rden", [128, 16])
        o_tok = sb("o_tok", [128, NB, E])
        oT = sb("oT", [128, 2, KC, S], F32R)
        x_res = sb("x_res", [128, NB, E])
        y = sb("y", [128, NB, E])
        stats = sb("stats", [128, NB, 6])
        mean_var = sb("mean_var", [128, NB, 2])
        var_eps = sb("var_eps", [128, NB])
        rstd = sb("rstd", [128, NB])
        x1T = sb("x1T", [128, 2, KC, S], F32R)
        gate = sb("gate", [128, 3, S])
        c2 = sb("c2", [128, KC, S])
        cT = sb("cT", [128, 2, KC, S], F32R)
        cu = sb("cu", [128, 2, NB, E], F32R)
        bias_raw = sb("bias_raw", [128, 3, KC])
        bias_half = sb("bias_half", [128, 2, KC])
        inc_sb = sb("inc_sb", [128, KC])
        bo_sb = sb("bo_sb", [128, E])
        minus_half = sb("minus_half", [128, NB])
        ident = sb("ident", [128, 128])
        ident_bf = sb("ident_bf", [128, 128], BF16)
        ident_r = sb("ident_r", [128, 128], F32R)
        mask = sb("mask", [128, 2, S], BF16)
        pos_raw = sb("pos_raw", [H, S])
        pos_parts = sb("pos_parts", [H, 2, S], F32R)
        tiles_raw = sb("tiles_raw", [N_TILES, 2, S])
        tiles_r = sb("tiles_r", [N_TILES, 2, S], F32R)

        banks = [ctx.enter_context(nc.psum_tensor(f"bank{i}", [128, S], F32)) for i in range(8)]
        MX, SC, CTX = banks[0:2], banks[2:4], banks[4]
        X, Y, Z = banks[5:8]

        x_hidden = gate[:, :, :]
        parts2 = (x1T, oT)
        ring = (x_res[:, :, :], y[:, :, :], o_tok[:, :, :],
                xt_raw[:, :, :].rearrange("p a b -> p (a b)").rearrange("p (n e) -> p n e", n=NB))

        x1_dram = nc.dram_tensor("x1_dram", [B, S, E], F32).ap()
        parts_dram = nc.dram_tensor("parts_dram", [2, 2, H // 2, 2, D, S], F32).ap()
        tok = "(n p) e -> p n e"

        weights_in, small_in, pos_in = sem("weights_in"), sem("small_in"), sem("pos_in")
        weights2_in = sem("weights2_in")
        xt_in, xres_in, x1_out, x1_in = sem("xt_in"), sem("xres_in"), sem("x1_out"), [sem(f"x1_in{i}") for i in range(4)]
        parts_out = [sem(f"parts_out{c}") for c in range(2)]
        stacked = [sem(f"stacked{c}") for c in range(2)]
        maxrow = [sem(f"maxrow{g}") for g in range(QUADS)]
        posrow = sem("posrow")
        out_sem = [sem("out0"), sem("out1")]
        const_ready, const_step, mem_ready, w_hi, w_lo, c_init = (
            sem("const_ready"), sem("const_step"), sem("mem_ready"), sem("w_hi"), sem("w_lo"), sem("c_init"))
        pos_split = sem("pos_split")
        waits_passed = sem("waits_passed")
        bias_ready = sem("bias_ready")
        mx_ready, sc_ready, mt_ready, pv_ready, ct_ready, v_ready, qk_ready, ot_ready, op_ready, xt_ready, f_ready = (
            sem(n) for n in ("mx_ready", "sc_ready", "mt_ready", "pv_ready", "ct_ready", "v_ready", "qk_ready",
                             "ot_ready", "op_ready", "xt_ready", "f_ready"))
        exp_done, ctx_done, maxrow_done, v_done, qkhi_done, othi_done, x1hi_done, gate_done, chi_done, xhi_done = (
            sem(n) for n in ("exp_done", "ctx_done", "maxrow_done", "v_done", "qkhi_done", "othi_done", "x1hi_done",
                             "gate_done", "chi_done", "xhi_done"))
        red_done, rden_done, o_done, qklo_done, otlo_done, y_done, stat_done, mv_done, x1_done = (
            sem(n) for n in ("red_done", "rden_done", "o_done", "qklo_done", "otlo_done", "y_done",
                             "stat_done", "mv_done", "x1_done"))
        x1lo_done, fc_done, c_done, clo_done, xlo_done = (
            sem(n) for n in ("x1lo_done", "fc_done", "c_done", "clo_done", "xlo_done"))
        masked_done, vareps_done, rstd_done = sem("masked_done"), sem("vareps_done"), sem("rstd_done")
        cu_ready, cu_sum, cuhi_done, culo_done = sem("cu_ready"), sem("cu_sum"), sem("cuhi_done"), sem("culo_done")
        t2_ready, t2hi, t2lo, o2_ready, h_done, z_done, st2, mv2, ve2, rs2, fin2 = (
            sem(n) for n in ("t2_ready", "t2hi", "t2lo", "o2_ready", "h_done", "z_done", "st2", "mv2", "ve2", "rs2", "fin2"))

        block = ctx.enter_context(nc.Block())

        own_wait = (nc.gpsimd.engine, nc.sync.engine)

        def real(t):
            return not isinstance(t, int) or 0 <= t < B

        def wait(eng, s, per, t, k):
            if isinstance(t, int):
                if t < 0:
                    return
                k, t = (per, B - 1) if t >= B else (k, t)
                if per * t + k <= 0:
                    return
            eng.wait_ge(s, per * t + k)
            if not isinstance(t, int) and eng.engine in own_wait:
                stand_alone(eng)

        def stand_alone(eng):
            eng.sem_inc(waits_passed, 1)

        def before(t, g):
            return (t, g - 1) if g else (t - 1, QUADS - 1)

        def freed(eng, t, *users):
            for s, per, dt, k in (users if isinstance(t, int) else users[:1]):
                wait(eng, s, per, t + dt, k)

        def head(g, hh):
            h = 4 * g + hh
            return 64 * (h % 2), h // 2

        def steps(eng, step, last=B):
            step(0, 0, 0)
            step(1, 0, 1)
            rounds = (last - 2) // 4
            with eng.Fori(0, rounds) as r:
                for i in range(4):
                    step(4 * r + (2 + i), r + (2 + i) // 4, (2 + i) % 4)
            for t in range(4 * rounds + 2, B):
                step(t, t // 4, t % 4)

        @block.sync
        def _(sp):
            v = "(c p) n -> p c n"
            w_stage = Pt[:, :, :].rearrange("p a b -> p (a b)")
            sp.dma_start(w_stage[:, 0:1536].rearrange("p (c n) -> p c n", c=KC), w_in.rearrange(v, p=128)).then_inc(weights_in, 16)
            sp.dma_start(xt_raw[:, :, :], xt[0].rearrange("(c p) s -> p c s", p=128)).then_inc(xt_in, 16)
            sp.dma_start(w_stage[:, 1536:2048].rearrange("p (c n) -> p c n", c=KC), w_out.rearrange(v, p=128)).then_inc(weights_in, 16)
            sp.dma_start(w_stage[:, 2048:3584].rearrange("p (c n) -> p c n", c=KC), w_gates.rearrange(v, p=128)).then_inc(weights_in, 16)
            sp.dma_start(w_stage[:, 3584:4096].rearrange("p (c n) -> p c n", c=KC), w_o.rearrange(v, p=128)).then_inc(weights_in, 16)
            sp.dma_start(gate[:, :, :].rearrange("p a b -> p (a b)").rearrange("p (c n) -> p c n", c=KC),
                         u_gates.rearrange(v, p=128)).then_inc(weights2_in, 16)
            sp.dma_start(ctx_raw[:, :].rearrange("p (c n) -> p c n", c=KC), u_o.rearrange(v, p=128)).then_inc(weights2_in, 16)
            sp.dma_start(pos_raw[:, :], pos_bias).then_inc(pos_in, 16)
            sp.dma_start(tiles_raw[:, :, :], tile_rows).then_inc(pos_in, 16)
            sp.dma_start(bias_raw[:, :, :], b_gates).then_inc(small_in, 16)
            sp.dma_start(inc_sb[:, :], in_c).then_inc(small_in, 16)
            sp.dma_start(bo_sb[:, :], b_o).then_inc(small_in, 16)
            sp.wait_ge(pos_split, 2)
            sp.wait_ge(mem_ready, 3)
            for par in range(2):
                for part in range(2):
                    r = 64 * par + ROW_BIAS + part
                    for b in range(H // 2):
                        h = 2 * b + par
                        sp.dma_start(Ks[r:r + 1, b, :].bitcast(F32), pos_parts[h:h + 1, part, :].bitcast(F32)).then_inc(posrow, 16)

            for par in range(2):
                for b in range(H // 2):
                    r = 64 * par + ROW_TILE
                    for which, dst in enumerate((Qs, Ks)):
                        sp.dma_start(dst[r:r + N_TILES, b, :].bitcast(F32), tiles_r[:, which, :].bitcast(F32)).then_inc(posrow, 16)

            def parts_to_dram(t, c):
                wait(sp, stacked[c], 16 * STACK_DMAS, t - 1, 16 * STACK_DMAS)
                for which in range(2):
                    wait(sp, qklo_done, 4, t, 2 * c + which + 1)
                    for part in range(2):
                        sp.dma_start(parts_dram[c, which, :, part, :, :],
                                     qk_parts[:, c, which, part, :].bitcast(F32)).then_inc(parts_out[c], 16)

            def stack(t, c):
                wait(sp, sc_ready, 32, t - 1, 16 * c + 16)
                wait(sp, parts_out[c], 64, t, 64)
                for which, (dst, groups) in enumerate(((Qs, ROWS_Q), (Ks, ROWS_K))):
                    src = parts_dram[c, which].rearrange("(b o) l d s -> o (l d) b s", o=2)
                    for odd in range(2):
                        for r, part, n in groups:
                            sp.dma_start(dst[64 * odd + r:64 * odd + r + n * D, 4 * c:4 * c + 4, :].bitcast(F32),
                                         src[odd, part * D:(part + n) * D, :, :]).then_inc(stacked[c], 16)

            def max_to_stack(t, g):
                wait(sp, maxrow_done, 4, t, g + 1)
                for odd in range(2):
                    r = 64 * odd + ROW_MAX
                    sp.dma_start(Qs[r:r + 1, 2 * g:2 * g + 2, :].bitcast(F32),
                                 max_rows[8 * odd:8 * odd + 8, :].bitcast(F32)).then_inc(maxrow[g], 16)

            def iteration(t):
                if real(t + 1):
                    wait(sp, xlo_done, 1, t, 1)
                    sp.dma_start(xt_raw[:, :, :], xt[t + 1].rearrange("(c p) s -> p c s", p=128)).then_inc(xt_in, 16)
                if real(t - 1):
                    wait(sp, y_done, 2, t - 2, 2)
                    sp.dma_start(x_res[:, :, :], x[t - 1].rearrange(tok, p=128)).then_inc(xres_in, 16)
                if real(t):
                    max_to_stack(t, 0)
                    parts_to_dram(t, 1)
                    stack(t, 1)
                    max_to_stack(t, 1)
                if real(t - 1):
                    wait(sp, x1_done, 4, t - 1, 4)
                    sp.dma_start(x1_dram[t - 1].rearrange(tok, p=128), y[:, :, :]).then_inc(x1_out, 16)
                if real(t):
                    if real(t + 1):
                        parts_to_dram(t + 1, 0)
                    max_to_stack(t, 2)
                    if real(t + 1):
                        stack(t + 1, 0)
                    max_to_stack(t, 3)

            parts_to_dram(0, 0)
            stack(0, 0)
            iteration(0)
            iteration(1)
            with sp.Fori(2, B - 1) as t:
                iteration(t)
            iteration(B - 1)
            iteration(B)
            iteration(B + 1)

            sp.wait_ge(x1_out, 16 * B)
            sp.wait_ge(xt_ready, 2 * B)
            def load(t, i):
                sp.dma_start(ring[i], x1_dram[t].rearrange(tok, p=128)).then_inc(x1_in[i], 16)

            def move(t, rnd, i):
                if not isinstance(t, int) or t + 4 < B:
                    sp.wait_ge(z_done, t + 1)
                    stand_alone(sp)
                    load(t + 4, i)
                sp.wait_ge(fin2, 4 * t + 4)
                stand_alone(sp)
                sp.dma_start(out[t].rearrange(tok, p=128), Pt[:, i % 2, :].rearrange("p (n e) -> p n e", n=NB)).then_inc(out_sem[i % 2], 16)

            for i in range(4):
                load(i, i)
            steps(sp, move, B - 4)
            sp.wait_ge(out_sem[0], 16 * B // 2)
            sp.wait_ge(out_sem[1], 16 * B // 2)

        @block.gpsimd
        def _(pool):
            gp = nc.gpsimd
            gp.memset(ident[:, :], 0.0).then_inc(const_step, 1)
            gp.memset(mask[:, :, :], 0.0).then_inc(const_step, 1)
            gp.memset(minus_half[:, :], -0.5).then_inc(const_step, 1)
            pool.wait_ge(const_step, 3)
            gp.affine_select(out=ident[:, :], in_=ident[:, :], compare_op=ALU.not_equal, fill=1.0, base=0,
                             pattern=[[-1, 128]], channel_multiplier=1).then_inc(const_step, 1)
            m4 = mask[:, :, :].rearrange("p a (b c) -> p (a b) c", c=256)
            gp.affine_select(out=m4[:, :, 128:256], in_=m4[:, :, 128:256], compare_op=ALU.is_ge, fill=MASKED, base=0,
                             pattern=[[0, 4], [-1, 128]], channel_multiplier=1).then_inc(const_step, 1)
            gp.affine_select(out=m4[:, 1:4, 0:128], in_=m4[:, 1:4, 0:128], compare_op=ALU.is_ge, fill=MASKED, base=0,
                             pattern=[[0, 3], [1, 128]], channel_multiplier=-1).then_inc(const_step, 1)
            gp.memset(m4[:, 0, 0:128], MASKED).then_inc(const_step, 1)
            pool.wait_ge(const_step, 7)
            gp.tensor_copy(ident_bf[:, :], ident[:, :]).then_inc(const_ready, 1)
            gp.tensor_copy(ident_r[:, :], ident[:, :]).then_inc(const_ready, 1)

            def window(t, g, hh):
                p4 = Pt[:, hh, :].rearrange("p (j c) -> p j c", c=256)
                wait(pool, exp_done, 32, t, 8 * g + 2 * hh + 2)
                gp.affine_select(out=p4[:, :, 0:128], in_=p4[:, :, 0:128], compare_op=ALU.is_ge, fill=0.0, base=0,
                                 pattern=[[0, 4], [1, 128]], channel_multiplier=-1)
                gp.affine_select(out=p4[:, 0:3, 128:256], in_=p4[:, 0:3, 128:256], compare_op=ALU.is_ge, fill=0.0, base=0,
                                 pattern=[[0, 3], [-1, 128]], channel_multiplier=1).then_inc(masked_done, 1)

            def inverse_std(t):
                wait(pool, mv_done, 4, t, 4)
                gp.tensor_scalar(var_eps[:, :], mean_var[:, :, 1], EPS, None, ALU.add).then_inc(vareps_done, 1)
                wait(pool, vareps_done, 1, t, 1)
                wait(pool, x1_done, 4, t - 1, 4)
                gp.tensor_tensor(rstd[:, :], var_eps[:, :], minus_half[:, :], ALU.pow).then_inc(rstd_done, 1)

            def iteration(t):
                for g in range(QUADS):
                    pt, pg = before(t, g)
                    if real(pt):
                        for hh in range(4):
                            window(pt, pg, hh)
                    if g == 1 and real(t - 1):
                        inverse_std(t - 1)

            iteration(0)
            iteration(1)
            with pool.Fori(2, B - 1) as t:
                iteration(t)
            iteration(B - 1)
            iteration(B)

            def second(t):
                pool.wait_ge(mv2, 4 * t + 4)
                stand_alone(pool)
                gp.tensor_scalar(var_eps[:, :], mean_var[:, :, 1], EPS, None, ALU.add).then_inc(ve2, 1)
                pool.wait_ge(ve2, t + 1)
                stand_alone(pool)
                gp.tensor_tensor(rstd[:, :], var_eps[:, :], minus_half[:, :], ALU.pow).then_inc(rs2, 1)

            with pool.Fori(0, B) as t:
                second(t)

        @block.scalar
        def _(act):
            sc = nc.scalar
            w_stage = Pt[:, :, :].rearrange("p a b -> p (a b)")
            act.wait_ge(pos_in, 32)
            sc.activation(tiles_r[:, :, :], tiles_raw[:, :, :], ACT.Copy).then_inc(pos_split, 1)
            sc.activation(pos_parts[:, 0, :], pos_raw[:, :], ACT.Copy).then_inc(w_hi, 1)
            act.wait_ge(weights_in, 64)
            act.wait_ge(weights2_in, 32)
            for dst, src in ((Win, w_stage[:, 0:1536]), (Wout, w_stage[:, 1536:2048]), (Wg, w_stage[:, 2048:3584]),
                             (Wo, w_stage[:, 3584:4096]), (Ug, gate[:, :, :].rearrange("p a b -> p (a b)")),
                             (Uo, ctx_raw[:, :])):
                sc.activation(dst[:, 0, :, :].rearrange("p a b -> p (a b)"), src, ACT.Copy).then_inc(w_hi, 1)

            def x_hi(t):
                wait(act, xt_in, 16, t, 16)
                wait(act, v_ready, 2, t - 1, 2)
                sc.activation(xT[:, 0, :, :], xt_raw[:, :, :], ACT.Copy).then_inc(xhi_done, 1)

            def qk_hi(t, k, bank):
                if k % 2 == 0:
                    wait(act, parts_out[k // 2], 64, t - 1, 64)
                wait(act, qk_ready, 4, t, k + 1)
                sc.activation(qk_parts[:, k // 2, k % 2, 0, :], bank[:, :], ACT.Copy,
                              scale=float(D) ** -0.5 if k % 2 == 0 else 1.0).then_inc(qkhi_done, 1)

            def v_out(t, half, bank):
                if half == 0:
                    wait(act, pv_ready, 4, t - 1, 4)
                wait(act, v_ready, 2, t, half + 1)
                sc.activation(Vp[:, 2 * half:2 * half + 2, 0:H * PITCH].rearrange("p n (h d) -> p n h d", d=PITCH)[:, :, :, 0:D],
                              bank[:, :].rearrange("p (n h d) -> p n h d", n=2, h=H), ACT.Copy).then_inc(v_done, 1)

            def exps(t, g, hh):
                if hh == 0:
                    wait(act, pv_ready, 4, t, g)
                for a, n in enumerate((S, S - WIN)):
                    wait(act, sc_ready, 32, t, 8 * g + 2 * hh + a + 1)
                    sc.activation(Pt[:, hh, S * a:S * a + n], SC[a][:, 0:n], ACT.Exp).then_inc(exp_done, 1)

            def max_row(t, g):
                pt, pg = before(t, g)
                wait(act, maxrow[pg], 16 * MAXROW_DMAS, pt, 16 * MAXROW_DMAS)
                wait(act, mt_ready, 4, t, g + 1)
                sc.activation(max_rows[:, :], CTX[0:16, 0:128], ACT.Copy, scale=-1.0).then_inc(maxrow_done, 1)

            def ctx_out(t, g):
                wait(act, pv_ready, 4, t, g + 1)
                wait(act, ct_ready, 4, t, g)
                sc.activation(ctx_raw[:, :], CTX[:, :], ACT.Copy).then_inc(ctx_done, 1)

            def ot_hi(t, c, bank):
                if c == 0:
                    wait(act, op_ready, 2, t - 1, 2)
                wait(act, ot_ready, 2, t, c + 1)
                sc.activation(oT[:, 0, c, :], bank[:, :], ACT.Copy).then_inc(othi_done, 1)

            def x1_hi(t, c, bank):
                if c == 0:
                    wait(act, f_ready, 6, t - 1, 6)
                wait(act, xt_ready, 2, t, c + 1)
                sc.activation(x1T[:, 0, c, :], bank[:, :], ACT.Copy).then_inc(x1hi_done, 1)

            def gates(t, k, bank):
                j, which = k // 3, k % 3
                wait(act, c_done, 2, t, j)
                wait(act, f_ready, 6, t, k + 1)
                if which < 2:
                    ins = sc.activation(gate[:, which, :], bank[:, :], ACT.Tanh, bias=bias_half[:, which, j:j + 1], scale=0.5)
                else:
                    ins = sc.activation(gate[:, which, :], bank[:, :], ACT.Tanh, bias=bias_raw[:, which, j:j + 1])
                ins.then_inc(gate_done, 1)

            def c_hi(t):
                wait(act, f_ready, 6, t, 6)
                for j in range(KC):
                    wait(act, c_done, 2, t, j + 1)
                    sc.activation(cT[:, 0, j, :], c2[:, j, :], ACT.Copy, scale=0.5).then_inc(chi_done, 1)

            def iteration(t):
                b3, p1, p2, n1, now = real(t - 1), real(t - 1), real(t - 2), real(t + 1), real(t)
                if b3: exps(t - 1, 3, 0)
                if p2: gates(t - 2, 4, Y)
                if b3: exps(t - 1, 3, 1)
                if p2: gates(t - 2, 5, Z)
                if p2: c_hi(t - 2)
                if b3: exps(t - 1, 3, 2)
                if now: qk_hi(t, 2, X)
                if b3: exps(t - 1, 3, 3)
                if now: max_row(t, 0)
                if now: qk_hi(t, 3, Y)
                if b3: ctx_out(t - 1, 3)

                if now: exps(t, 0, 0)
                if now: v_out(t, 0, X)
                if now: exps(t, 0, 1)
                if now: v_out(t, 1, Y)
                if n1: x_hi(t + 1)
                if now: exps(t, 0, 2)
                if p1:
                    ot_hi(t - 1, 0, Z)
                    ot_hi(t - 1, 1, X)
                if now:
                    exps(t, 0, 3)
                    max_row(t, 1)
                    ctx_out(t, 0)

                if now:
                    exps(t, 1, 0)
                    exps(t, 1, 1)
                if n1: qk_hi(t + 1, 0, Y)
                if now: exps(t, 1, 2)
                if n1: qk_hi(t + 1, 1, Z)
                if now: exps(t, 1, 3)
                if p1:
                    x1_hi(t - 1, 0, X)
                    x1_hi(t - 1, 1, Y)
                if now: max_row(t, 2)
                if p1: gates(t - 1, 0, Z)
                if now:
                    ctx_out(t, 1)

                    exps(t, 2, 0)
                    exps(t, 2, 1)
                if p1: gates(t - 1, 1, Y)
                if now: exps(t, 2, 2)
                if p1: gates(t - 1, 2, Z)
                if now: exps(t, 2, 3)
                if now: max_row(t, 3)
                if p1: gates(t - 1, 3, X)
                if now: ctx_out(t, 2)

            act.wait_ge(bias_ready, 1)
            x_hi(0)
            act.wait_ge(c_init, 1)
            for j in range(KC):
                sc.activation(cT[:, 0, j, :], c2[:, j, :], ACT.Copy, scale=0.5).then_inc(w_hi, 1)
            act.wait_ge(w_lo, 7)
            qk_hi(0, 0, Y)
            qk_hi(0, 1, Z)
            iteration(0)
            iteration(1)
            with act.Fori(2, B - 1) as t:
                iteration(t)
            iteration(B - 1)
            iteration(B)
            iteration(B + 1)

            for a in range(2):
                act.wait_ge(cu_sum, a + 1)
                sc.activation(cu[:, 0, 2 * a:2 * a + 2, :], x_hidden[:, a, :].rearrange("p (n e) -> p n e", n=2), ACT.Copy).then_inc(cuhi_done, 1)

            def hi2(t, i):
                if not isinstance(t, int) or t >= 2:
                    act.wait_ge(o2_ready, 2 * t - 2)
                for c in range(KC):
                    act.wait_ge(t2_ready, 2 * t + (c + 1))
                    sc.activation(parts2[i][:, 0, c, :], banks[2 * i + c][:, :], ACT.Copy).then_inc(t2hi, 1)

            def hidden(t, rnd, i):
                if not isinstance(t, int) or t + 1 < B:
                    hi2(t + 1, (i + 1) % 2)
                if not isinstance(t, int) or t >= 2:
                    act.wait_ge(z_done, t - 1)
                for a in range(2):
                    act.wait_ge(o2_ready, 2 * t + (a + 1))
                    sc.activation(Pt[:, 2 + i % 2, S * a:S * a + S], banks[4 + 2 * (i % 2) + a][:, :], ACT.Tanh).then_inc(h_done, 1)

            hi2(0, 0)
            steps(act, hidden)

        @block.vector
        def _(dve):
            ve = nc.vector

            def minus_hi(out_, in_, hi, scale=1.0):
                return ve.scalar_tensor_tensor(out_, in_, scale, hi.bitcast(F32), op0=ALU.mult, op1=ALU.subtract)

            w_stage = Pt[:, :, :].rearrange("p a b -> p (a b)")
            ve.memset(Qs[:, :, :].bitcast(F32), 1.0).then_inc(mem_ready, 1)
            ve.memset(Ks[:, :, :].bitcast(F32), 1.0).then_inc(mem_ready, 1)
            ve.memset(Vp[:, :, :], 1.0).then_inc(mem_ready, 1)
            ve.memset(c2[:, :, :], 2.0).then_inc(mem_ready, 1)
            dve.wait_ge(w_hi, 1)
            minus_hi(pos_parts[:, 1, :], pos_raw[:, :], pos_parts[:, 0, :]).then_inc(pos_split, 1)
            dve.wait_ge(small_in, 48)
            ve.tensor_scalar(bias_half[:, :, :], bias_raw[:, 0:2, :], 0.5, None, ALU.mult).then_inc(bias_ready, 1)
            dve.wait_ge(mem_ready, 4)
            for j in range(KC):
                ins = ve.tensor_scalar(c2[:, j, :], c2[:, j, :], inc_sb[:, j:j + 1], None, ALU.mult)
            ins.then_inc(c_init, 1)
            for n, (dst, src) in enumerate(((Win, w_stage[:, 0:1536]), (Wout, w_stage[:, 1536:2048]), (Wg, w_stage[:, 2048:3584]),
                                            (Wo, w_stage[:, 3584:4096]), (Ug, gate[:, :, :].rearrange("p a b -> p (a b)")),
                                            (Uo, ctx_raw[:, :]))):
                dve.wait_ge(w_hi, n + 2)
                minus_hi(dst[:, 1, :, :].rearrange("p a b -> p (a b)"), src,
                         dst[:, 0, :, :].rearrange("p a b -> p (a b)")).then_inc(w_lo, 1)

            def x_lo(t):
                wait(dve, xhi_done, 1, t, 1)
                minus_hi(xT[:, 1, :, :], xt_raw[:, :, :], xT[:, 0, :, :]).then_inc(xlo_done, 1)

            def qk_lo(t, k, bank):
                wait(dve, qkhi_done, 4, t, k + 1)
                minus_hi(qk_parts[:, k // 2, k % 2, 1, :], bank[:, :], qk_parts[:, k // 2, k % 2, 0, :],
                         float(D) ** -0.5 if k % 2 == 0 else 1.0).then_inc(qklo_done, 1)

            def maxima(t, g, hh):
                if hh == 0:
                    wait(dve, mt_ready, 4, t, g)
                for a in range(2):
                    wait(dve, mx_ready, 32, t, 8 * g + 2 * hh + a + 1)
                    at = 8 * (hh % 2) + 4 * (hh // 2) + 2 * a
                    ve.tensor_reduce(out=max_q[:, at:at + 2],
                                     in_=MX[a][:, :].rearrange("p (n k) -> p n k", n=2), axis=AX.X, op=ALU.max).then_inc(red_done, 1)

            def normalise(t, g, bank):
                c4 = bank[:, :].rearrange("p (n h d) -> p n h d", n=NB, h=4)
                wait(dve, ct_ready, 4, t, g + 1)
                wait(dve, o_done, 4, t, g)
                ve.reciprocal(rden[:, :].rearrange("p (n h) -> p n h", n=NB), c4[:, :, :, D]).then_inc(rden_done, 1)
                wait(dve, rden_done, 4, t, g + 1)
                wait(dve, ot_ready, 2, t - 1, 2)
                o4 = o_tok[:, :, 4 * D * g:4 * D * (g + 1)].rearrange("p n (h d) -> p n h d", h=4)
                r4 = rden[:, :].rearrange("p (n h) -> p n h", n=NB).unsqueeze(3).to_broadcast([128, NB, 4, D])
                ve.tensor_tensor(o4, c4[:, :, :, 0:D], r4, ALU.mult).then_inc(o_done, 1)

            def ot_lo(t, c, bank):
                wait(dve, othi_done, 2, t, c + 1)
                minus_hi(oT[:, 1, c, :], bank[:, :], oT[:, 0, c, :]).then_inc(otlo_done, 1)

            def residual(t, half, bank):
                if half == 0:
                    wait(dve, xres_in, 16, t, 16)
                    wait(dve, xt_ready, 2, t - 1, 2)
                    wait(dve, x1_out, 16, t - 1, 16)
                wait(dve, op_ready, 2, t, half + 1)
                ve.tensor_tensor(y[:, 2 * half:2 * half + 2, :], bank[:, :].rearrange("p (n e) -> p n e", n=2),
                                 x_res[:, 2 * half:2 * half + 2, :], ALU.add).then_inc(y_done, 1)

            def statistics(t):
                for n in range(NB):
                    wait(dve, y_done, 2, t, n // 2 + 1)
                    ve.bn_stats(stats[:, n, :], y[:, n, :]).then_inc(stat_done, 1)
                for n in range(NB):
                    wait(dve, stat_done, 4, t, n + 1)
                    stand_alone(dve)
                    ve.bn_aggr(mean_var[:, n, :], stats[:, n, :]).then_inc(mv_done, 1)

            def layernorm(t):
                wait(dve, rstd_done, 1, t, 1)
                for n in range(NB):
                    ve.tensor_scalar(y[:, n, :], y[:, n, :], mean_var[:, n, 0:1], rstd[:, n:n + 1],
                                     ALU.subtract, ALU.mult).then_inc(x1_done, 1)

            def x1_lo(t, c, bank):
                wait(dve, x1hi_done, 2, t, c + 1)
                minus_hi(x1T[:, 1, c, :], bank[:, :], x1T[:, 0, c, :]).then_inc(x1lo_done, 1)

            def update(t, j):
                wait(dve, gate_done, 6, t, 3 * j + 3)
                if j == 0:
                    wait(dve, chi_done, 2, t - 1, 2)
                ve.scalar_tensor_tensor(gate[:, 0, :], gate[:, 0, :], 1.0, c2[:, j, :], op0=ALU.add, op1=ALU.mult).then_inc(fc_done, 1)
                ve.scalar_tensor_tensor(gate[:, 1, :], gate[:, 1, :], 1.0, gate[:, 2, :], op0=ALU.add, op1=ALU.mult).then_inc(fc_done, 1)
                wait(dve, fc_done, 4, t, 2 * j + 2)
                ve.scalar_tensor_tensor(c2[:, j, :], gate[:, 0, :], 0.5, gate[:, 1, :], op0=ALU.mult, op1=ALU.add).then_inc(c_done, 1)

            def c_lo(t):
                for j in range(KC):
                    wait(dve, chi_done, 2, t, j + 1)
                    minus_hi(cT[:, 1, j, :], c2[:, j, :], cT[:, 0, j, :], 0.5).then_inc(clo_done, 1)

            def iteration(t):
                p1, p2, n1, now = real(t - 1), real(t - 2), real(t + 1), real(t)
                if now: maxima(t, 0, 0)
                if p1: normalise(t - 1, 2, X)
                if now: maxima(t, 0, 1)
                if p2:
                    update(t - 2, 1)
                if now: maxima(t, 0, 2)
                if p2: c_lo(t - 2)
                if now:
                    qk_lo(t, 2, X)
                    maxima(t, 0, 3)
                    qk_lo(t, 3, Y)

                    maxima(t, 1, 0)
                if p1: normalise(t - 1, 3, Z)
                if now:
                    maxima(t, 1, 1)
                    maxima(t, 1, 2)
                if n1: x_lo(t + 1)
                if p1:
                    ot_lo(t - 1, 0, Z)
                    ot_lo(t - 1, 1, X)
                if now: maxima(t, 1, 3)
                if p1: residual(t - 1, 0, Y)
                if p1:
                    residual(t - 1, 1, Z)
                    statistics(t - 1)

                if now:
                    maxima(t, 2, 0)
                    normalise(t, 0, X)
                    maxima(t, 2, 1)
                if p1: layernorm(t - 1)
                if n1: qk_lo(t + 1, 0, Y)
                if now: maxima(t, 2, 2)
                if n1: qk_lo(t + 1, 1, Z)
                if now: maxima(t, 2, 3)
                if p1:
                    x1_lo(t - 1, 0, X)
                    x1_lo(t - 1, 1, Y)
                if now:

                    maxima(t, 3, 0)
                    normalise(t, 1, X)
                    maxima(t, 3, 1)
                    maxima(t, 3, 2)
                if p1: update(t - 1, 0)
                if now:
                    maxima(t, 3, 3)

            x_lo(0)
            for j in range(KC):
                dve.wait_ge(w_hi, 8 + j)
                minus_hi(cT[:, 1, j, :], c2[:, j, :], cT[:, 0, j, :], 0.5).then_inc(w_lo, 1)
            qk_lo(0, 0, Y)
            qk_lo(0, 1, Z)
            iteration(0)
            iteration(1)
            with dve.Fori(2, B - 1) as t:
                iteration(t)
            iteration(B - 1)
            iteration(B)
            iteration(B + 1)

            for a in range(2):
                dve.wait_ge(cu_ready, a + 1)
                ve.tensor_tensor(x_hidden[:, a, :].rearrange("p (n e) -> p n e", n=2), banks[a][:, :].rearrange("p (n e) -> p n e", n=2),
                                 bo_sb[:, :].unsqueeze(1).to_broadcast([128, 2, E]), ALU.add).then_inc(cu_sum, 1)
            for a in range(2):
                dve.wait_ge(cuhi_done, a + 1)
                minus_hi(cu[:, 1, 2 * a:2 * a + 2, :], x_hidden[:, a, :].rearrange("p (n e) -> p n e", n=2),
                         cu[:, 0, 2 * a:2 * a + 2, :]).then_inc(culo_done, 1)
            def lo2(t, i):
                for c in range(KC):
                    dve.wait_ge(t2hi, 2 * t + (c + 1))
                    minus_hi(parts2[i][:, 1, c, :], banks[2 * i + c][:, :], parts2[i][:, 0, c, :]).then_inc(t2lo, 1)

            def finish(t, rnd, i):
                if not isinstance(t, int) or t + 1 < B:
                    lo2(t + 1, (i + 1) % 2)
                if not isinstance(t, int) or t >= 2:
                    dve.wait_ge(out_sem[i % 2], 16 * 2 * rnd + (16 if i >= 2 else 0))
                z = Pt[:, i % 2, :].rearrange("p (n e) -> p n e", n=NB)
                dve.wait_ge(h_done, 2 * t + 2)
                ve.tensor_tensor(z, Pt[:, 2 + i % 2, :].rearrange("p (n e) -> p n e", n=NB), ring[i], ALU.add).then_inc(z_done, 1)
                dve.wait_ge(z_done, t + 1)
                for n in range(NB):
                    ve.bn_stats(stats[:, n, :], z[:, n, :]).then_inc(st2, 1)
                for n in range(NB):
                    dve.wait_ge(st2, 4 * t + (n + 1))
                    stand_alone(dve)
                    ve.bn_aggr(mean_var[:, n, :], stats[:, n, :]).then_inc(mv2, 1)
                dve.wait_ge(rs2, t + 1)
                for n in range(NB):
                    ve.tensor_scalar(z[:, n, :], z[:, n, :], mean_var[:, n, 0:1], rstd[:, n:n + 1],
                                     ALU.subtract, ALU.mult).then_inc(fin2, 1)

            lo2(0, 0)
            steps(dve, finish)

        @block.tensor
        def _(pe):
            te = nc.tensor
            PASSES = ((0, 0), (0, 1), (1, 0))

            def product(out_, pairs, s):
                todo = [(w(a), m(b)) for w, m in pairs for a, b in PASSES]
                for n, (w, m) in enumerate(todo):
                    ins = te.matmul(out_, w, m, start=(n == 0), stop=(n == len(todo) - 1))
                if s is not None:
                    ins.then_inc(s, 1)

            def masked_scores(t, g, hh):
                base, blk = head(g, hh)
                if hh == 0:
                    wait(pe, stacked[g // 2], 16 * STACK_DMAS, t, 16 * STACK_DMAS)
                q, k = Qs[base:base + K_MAXIMA, blk, :], Ks[base:base + K_MAXIMA, blk, :]
                for a in range(2):
                    wait(pe, red_done, 32, t, 8 * g + 2 * hh + a - 1)
                    for n in (2 * a, 2 * a + 1):
                        lo = max(n - 1, 0) * WIN
                        width = (n + 1) * WIN - lo
                        end = 256 * (n % 2) + 256
                        te.matmul(MX[a][:, end - width:end], q[:, n * WIN:(n + 1) * WIN], k[:, lo:(n + 1) * WIN],
                                  start=(n % 2 == 0), stop=False, skip_group_check=True)
                    ins = te.matmul(MX[a][:, :], ident_bf[:, :], mask[:, a, :], start=False, stop=True, skip_group_check=True)
                    ins.then_inc(mx_ready, 1)

            def max_transpose(t, g):
                wait(pe, red_done, 32, t, 8 * g + 8)
                wait(pe, ctx_done, 4, t, g - 1)
                te.transpose(CTX[0:16, 0:128], max_q[:, :], ident[:, :]).then_inc(mt_ready, 1)

            def scores(t, g, hh):
                base, blk = head(g, hh)
                if hh == 0:
                    wait(pe, maxrow[g], 16 * MAXROW_DMAS, t, 16 * MAXROW_DMAS)
                q, k = Qs[base:base + K_SCORES, blk, :], Ks[base:base + K_SCORES, blk, :]
                for a in range(2):
                    wait(pe, exp_done, 32, t, 8 * g + 2 * hh + a - 1)
                    for j in (2 * a, 2 * a + 1):
                        width = min(2 * WIN, S - j * WIN)
                        ins = te.matmul(SC[a][:, 256 * (j % 2):256 * (j % 2) + width], k[:, j * WIN:(j + 1) * WIN],
                                        q[:, j * WIN:j * WIN + width], start=True, stop=True)
                    ins.then_inc(sc_ready, 1)

            def values(t, g, slot_t):
                wait(pe, masked_done, 16, t, 4 * g + 4)
                if g == 0:
                    wait(pe, v_done, 2, t, 2)
                nt, ng = (t, g + 1) if g < 3 else (slot_t, 0)
                if real(nt):
                    wait(pe, maxrow_done, 4, nt, ng + 1)
                else:
                    wait(pe, ctx_done, 4, t, g)
                for j in range(NB):
                    width = min(2 * WIN, S - j * WIN)
                    for hh in range(4):
                        h = 4 * g + hh
                        ins = te.matmul(CTX[32 * hh:32 * hh + 32, j * WIN:j * WIN + width], Vp[:, j, PITCH * h:PITCH * h + 32],
                                        Pt[:, hh, 256 * j:256 * j + width], start=(j == 0), stop=(j == NB - 1),
                                        skip_group_check=True)
                ins.then_inc(pv_ready, 1)

            def ctx_transpose(t, g, bank):
                wait(pe, ctx_done, 4, t, g + 1)
                for n in range(NB):
                    ins = te.transpose(bank[:, WIN * n:WIN * (n + 1)], ctx_raw[:, WIN * n:WIN * (n + 1)], ident[:, :])
                ins.then_inc(ct_ready, 1)

            def project_qk(t, k, bank):
                wait(pe, xlo_done, 1, t, 1)
                col = E * (k % 2) + 128 * (k // 2)
                product(bank[:, :], [(lambda a, c=c: Win[:, a, c, col:col + 128], lambda b, c=c: xT[:, b, c, :])
                                     for c in range(KC)], qk_ready)

            def project_v(t, half, bank):
                for n in (2 * half, 2 * half + 1):
                    product(bank[:, E * (n % 2):E * (n % 2) + E],
                            [(lambda a, c=c: xT[:, a, c, n * WIN:(n + 1) * WIN], lambda b, c=c: Win[:, b, c, 2 * E:3 * E])
                             for c in range(KC)], v_ready if n % 2 else None)

            def o_transpose(t, c, bank):
                wait(pe, o_done, 4, t, 4)
                for n in range(NB):
                    ins = te.transpose(bank[:, WIN * n:WIN * (n + 1)], o_tok[:, n, 128 * c:128 * c + 128], ident[:, :])
                ins.then_inc(ot_ready, 1)

            def project_out(t, half, bank):
                wait(pe, otlo_done, 2, t, 2)
                for n in (2 * half, 2 * half + 1):
                    product(bank[:, E * (n % 2):E * (n % 2) + E],
                            [(lambda a, c=c: oT[:, a, c, n * WIN:(n + 1) * WIN], lambda b, c=c: Wout[:, b, c, :])
                             for c in range(KC)], op_ready if n % 2 else None)

            def x1_transpose(t, c, bank):
                wait(pe, x1_done, 4, t, 4)
                for n in range(NB):
                    ins = te.transpose(bank[:, WIN * n:WIN * (n + 1)], y[:, n, 128 * c:128 * c + 128], ident[:, :])
                ins.then_inc(xt_ready, 1)

            def gate_product(t, k, bank):
                j, which = k // 3, k % 3
                wait(pe, x1lo_done, 2, t, 2)
                wait(pe, clo_done, 2, t - 1, 2)
                col = E * which + 128 * j
                product(bank[:, :],
                        [(lambda a, c=c: Wg[:, a, c, col:col + 128], lambda b, c=c: x1T[:, b, c, :]) for c in range(KC)]
                        + [(lambda a, c=c: Ug[:, a, c, col:col + 128], lambda b, c=c: cT[:, b, c, :]) for c in range(KC)],
                        f_ready)

            def iteration(t):
                p1, p2, n1, now = real(t - 1), real(t - 2), real(t + 1), real(t)

                def attend(g, hh):
                    if now:
                        masked_scores(t, g, hh)
                    pt, pg = before(t, g)
                    if real(pt):
                        scores(pt, pg, hh)

                attend(0, 0)
                if p1:
                    freed(pe, t, (gate_done, 6, -2, 4), (o_done, 4, -1, 2), (x1lo_done, 2, -2, 1))
                    ctx_transpose(t - 1, 2, X)
                if p2:
                    freed(pe, t, (gate_done, 6, -2, 2), (x1lo_done, 2, -2, 2), (qklo_done, 4, -1, 1))
                    gate_product(t - 2, 4, Y)
                attend(0, 1)
                if p2:
                    freed(pe, t, (gate_done, 6, -2, 3), (gate_done, 6, -2, 1))
                    gate_product(t - 2, 5, Z)
                attend(0, 2)
                if now:
                    freed(pe, t, (o_done, 4, -1, 3), (o_done, 4, -1, 2))
                    project_qk(t, 2, X)
                attend(0, 3)
                if now:
                    max_transpose(t, 0)
                    freed(pe, t, (gate_done, 6, -2, 5), (gate_done, 6, -2, 2), (qklo_done, 4, 0, 1))
                    project_qk(t, 3, Y)
                if p1:
                    values(t - 1, 3, t)
                attend(1, 0)
                if p1:
                    freed(pe, t, (gate_done, 6, -2, 6), (gate_done, 6, -2, 3), (qklo_done, 4, 0, 2))
                    ctx_transpose(t - 1, 3, Z)
                if now:
                    freed(pe, t, (qklo_done, 4, 0, 3))
                    project_v(t, 0, X)
                attend(1, 1)
                if now:
                    freed(pe, t, (qklo_done, 4, 0, 4))
                    project_v(t, 1, Y)
                attend(1, 2)
                if p1:
                    freed(pe, t, (o_done, 4, -1, 4))
                    o_transpose(t - 1, 0, Z)
                    freed(pe, t, (v_done, 2, 0, 1), (o_done, 4, -1, 3))
                    o_transpose(t - 1, 1, X)
                attend(1, 3)
                if p1:
                    freed(pe, t, (v_done, 2, 0, 2), (gate_done, 6, -2, 5))
                    project_out(t - 1, 0, Y)
                if now:
                    max_transpose(t, 1)
                if p1:
                    freed(pe, t, (otlo_done, 2, -1, 1))
                    project_out(t - 1, 1, Z)
                if now:
                    values(t, 0, t)
                attend(2, 0)
                if now:
                    freed(pe, t, (otlo_done, 2, -1, 2), (v_done, 2, 0, 1))
                    ctx_transpose(t, 0, X)
                attend(2, 1)
                if n1:
                    freed(pe, t, (y_done, 2, -1, 1), (v_done, 2, 0, 2))
                    project_qk(t + 1, 0, Y)
                attend(2, 2)
                if n1:
                    freed(pe, t, (y_done, 2, -1, 2), (qklo_done, 4, 0, 2))
                    project_qk(t + 1, 1, Z)
                attend(2, 3)
                if p1:
                    freed(pe, t, (o_done, 4, 0, 1), (otlo_done, 2, -1, 2))
                    x1_transpose(t - 1, 0, X)
                    freed(pe, t, (qklo_done, 4, 1, 1), (y_done, 2, -1, 1))
                    x1_transpose(t - 1, 1, Y)
                if now:
                    max_transpose(t, 2)
                if p1:
                    freed(pe, t, (qklo_done, 4, 1, 2), (y_done, 2, -1, 2))
                    gate_product(t - 1, 0, Z)
                if now:
                    values(t, 1, t)
                attend(3, 0)
                if now:
                    freed(pe, t, (x1lo_done, 2, -1, 1), (o_done, 4, 0, 1))
                    ctx_transpose(t, 1, X)
                attend(3, 1)
                if p1:
                    freed(pe, t, (x1lo_done, 2, -1, 2))
                    gate_product(t - 1, 1, Y)
                attend(3, 2)
                if p1:
                    freed(pe, t, (gate_done, 6, -1, 1))
                    gate_product(t - 1, 2, Z)
                attend(3, 3)
                if now:
                    max_transpose(t, 3)
                if p1:
                    freed(pe, t, (o_done, 4, 0, 2), (x1lo_done, 2, -1, 1))
                    gate_product(t - 1, 3, X)
                if now:
                    values(t, 2, t)

            pe.wait_ge(const_ready, 2)
            pe.wait_ge(w_lo, 8)
            pe.wait_ge(posrow, 16 * 4 * H)
            project_qk(0, 0, Y)
            project_qk(0, 1, Z)
            iteration(0)
            iteration(1)
            with pe.Fori(2, B - 1) as t:
                iteration(t)
            iteration(B - 1)
            iteration(B)
            iteration(B + 1)

            pe.wait_ge(clo_done, 2 * B)
            for n in range(NB):
                product(banks[n // 2][:, E * (n % 2):E * (n % 2) + E],
                        [(lambda a, c=c: cT[:, a, c, n * WIN:(n + 1) * WIN], lambda b, c=c: Uo[:, b, c, :])
                         for c in range(KC)], cu_ready if n % 2 else None)
            pe.wait_ge(cu_sum, 2)
            def transpose2(t, rnd, i):
                pe.wait_ge(x1_in[i], 16 * rnd + 16)
                if not isinstance(t, int) or t >= 2:
                    pe.wait_ge(t2lo, 2 * t - 2)
                for c in range(KC):
                    for n in range(NB):
                        ins = te.transpose(banks[2 * (i % 2) + c][:, WIN * n:WIN * (n + 1)], ring[i][:, n, 128 * c:128 * c + 128], ident[:, :])
                    ins.then_inc(t2_ready, 1)

            def output(t, rnd, i):
                if not isinstance(t, int) or t + 1 < B:
                    transpose2(t + 1, rnd + (i + 1) // 4, (i + 1) % 4)
                pe.wait_ge(t2lo, 2 * t + 2)
                if not isinstance(t, int) or t >= 2:
                    pe.wait_ge(h_done, 2 * t - 2)
                for a in range(2):
                    bank = banks[4 + 2 * (i % 2) + a]
                    for n in (2 * a, 2 * a + 1):
                        for c in range(KC):
                            for wa, wb in PASSES:
                                te.matmul(bank[:, E * (n % 2):E * (n % 2) + E], parts2[i % 2][:, wa, c, n * WIN:(n + 1) * WIN],
                                          Wo[:, wb, c, :], start=(n % 2 == 0 and c == 0 and (wa, wb) == PASSES[0]),
                                          stop=False, skip_group_check=True)
                    for part in range(2):
                        ins = te.matmul(bank[:, :], ident_r[:, :], cu[:, part, 2 * a:2 * a + 2, :].rearrange("p n e -> p (n e)"),
                                        start=False, stop=(part == 1), skip_group_check=True)
                    ins.then_inc(o2_ready, 1)

            transpose2(0, 0, 0)
            pe.wait_ge(culo_done, 2)
            steps(pe, output)


def kernel(L0_attn_x, L0_attn_w_in, L0_attn_w_out, L0_ffn_wf, L0_ffn_uf, L0_ffn_bf, L0_ffn_wi, L0_ffn_ui, L0_ffn_bi,
           L0_ffn_wc, L0_ffn_uc, L0_ffn_bc, L0_ffn_wo, L0_ffn_uo, L0_ffn_bo, L0_ffn_in_c):
    import concourse.bacc as bacc
    from concourse.bass_utils import run_bass_kernel_spmd

    def rows(a):
        return np.ascontiguousarray(a)

    slopes = np.exp2(-(np.arange(H, dtype=np.float32) + 1.0) * 8.0 / H).astype(np.float32)
    positions = np.arange(S, dtype=np.float32) - S // 2
    tile = np.arange(S) // 32
    behind = (tile[None, :] - np.arange(N_TILES)[:, None]) % N_TILES
    left_out = np.where(behind > 4, np.float32(MASKED), np.float32(0))
    in_tile = (tile[None, :] % N_TILES == np.arange(N_TILES)[:, None]).astype(np.float32)
    tile_rows = np.ascontiguousarray(np.stack([left_out, in_tile], axis=1).astype(np.float32))
    arrays = {
        "x": rows(L0_attn_x),
        "xt": rows(np.transpose(L0_attn_x, (0, 2, 1))),
        "w_in": rows(np.transpose(L0_attn_w_in)),
        "w_out": rows(np.transpose(L0_attn_w_out)),
        "w_gates": rows(np.concatenate([np.transpose(w) for w in (L0_ffn_wf, L0_ffn_wi, L0_ffn_wc)], axis=1)),
        "u_gates": rows(np.concatenate([np.transpose(w) for w in (L0_ffn_uf, L0_ffn_ui, L0_ffn_uc)], axis=1)),
        "b_gates": rows(np.transpose(np.reshape(np.stack([L0_ffn_bf, L0_ffn_bi, L0_ffn_bc]), (3, KC, 128)), (2, 0, 1))),
        "w_o": rows(np.transpose(L0_ffn_wo)),
        "u_o": rows(np.transpose(L0_ffn_uo)),
        "b_o": rows(np.broadcast_to(np.reshape(L0_ffn_bo, (1, E)), (128, E))),
        "in_c": rows(np.transpose(np.reshape(L0_ffn_in_c, (KC, 128)))),
        "pos_bias": -slopes[:, None] * positions[None, :],
        "tile_rows": tile_rows,
    }
    nc = bacc.Bacc("TRN2", target_bir_lowering=False, num_devices=1)
    args = [nc.dram_tensor(f"in_{n}", a.shape, mybir.dt.from_np(a.dtype), kind="ExternalInput").ap() for n, a in arrays.items()]
    result = nc.dram_tensor("result", (B, S, E), mybir.dt.float32, kind="ExternalOutput").ap()
    build(nc, *args, result)
    r = run_bass_kernel_spmd(nc, [{f"in_{n}": a for n, a in arrays.items()}], core_ids=[0])
    return r.results[0]["result"]
```

```python
import numpy as np
import concourse.bass as bass
from concourse import mybir
from contextlib import ExitStack

B, S, E = 16, 512, 256
H = 16
D = E // H
WIN = 128
NB = S // WIN
KC = E // 128
QUADS = H // 4
EPS = 1e-5
MASKED = -1e30

ROWS_Q = ((0, 0, 2), (2 * D, 0, 1))
ROWS_K = ((0, 0, 1), (D, 0, 2))
ROW_TILE = 3 * D
N_TILES = 8
ROW_BIAS = ROW_TILE + N_TILES
ROW_MAX = ROW_BIAS + 2
K_MAXIMA = ROW_MAX
K_SCORES = ROW_MAX + 1
PITCH = D + 1
VCOLS = H * PITCH + 16

STACK_DMAS = 8
PEELED = 6
MAXROW_DMAS = 2


def build(nc, x, xt, w_in, w_out, w_gates, u_gates, b_gates, w_o, u_o, b_o, in_c, pos_bias, tile_rows, out):
    F32, F32R, BF16 = mybir.dt.float32, mybir.dt.float32r, mybir.dt.bfloat16
    ACT, ALU, AX = mybir.ActivationFunctionType, mybir.AluOpType, mybir.AxisListType
    ctx = ExitStack()
    with ctx:
        def sb(name, shape, dt=F32):
            return ctx.enter_context(nc.sbuf_tensor(name, shape, dt))

        def sem(name):
            return ctx.enter_context(nc.semaphore(name))

        Win = sb("Win", [128, 2, KC, 3 * E], F32R)
        Wout = sb("Wout", [128, 2, KC, E], F32R)
        Wg = sb("Wg", [128, 2, KC, 3 * E], F32R)
        Ug = sb("Ug", [128, 2, KC, 3 * E], F32R)
        Wo = sb("Wo", [128, 2, KC, E], F32R)
        Uo = sb("Uo", [128, 2, KC, E], F32R)
        Qs = sb("Qs", [128, H // 2, S], F32R)
        Ks = sb("Ks", [128, H // 2, S], F32R)
        qk_parts = sb("qk_parts", [128, 2, 2, 2, S], F32R)
        Vp = sb("Vp", [128, NB, VCOLS])
        Pt = sb("Pt", [128, 4, 2 * S])
        xt_raw = sb("xt_raw", [128, KC, S])
        xT = sb("xT", [128, 2, KC, S], F32R)
        max_q = sb("max_q", [128, 16])
        max_rows = sb("max_rows", [16, 128], F32R)
        ctx_raw = sb("ctx_raw", [128, S])
        rden = sb("rden", [128, 16])
        o_tok = sb("o_tok", [128, NB, E])
        oT = sb("oT", [128, 2, KC, S], F32R)
        x_res = sb("x_res", [128, NB, E])
        y = sb("y", [128, NB, E])
        stats = sb("stats", [128, NB, 6])
        mean_var = sb("mean_var", [128, 2, NB, 2])
        var_eps = sb("var_eps", [128, NB])
        rstd = sb("rstd", [128, 2, NB])
        shift = sb("shift", [128, 2, NB])
        minus_mean = sb("minus_mean", [128, NB])
        x1T = sb("x1T", [128, 2, KC, S], F32R)
        gate = sb("gate", [128, 3, S])
        c2 = sb("c2", [128, KC, S])
        cT = sb("cT", [128, 2, KC, S], F32R)
        cu = sb("cu", [128, 2, NB, E], F32R)
        bias_raw = sb("bias_raw", [128, 3, KC])
        bias_half = sb("bias_half", [128, 2, KC])
        inc_sb = sb("inc_sb", [128, KC])
        bo_sb = sb("bo_sb", [128, E])
        minus_half = sb("minus_half", [128, NB])
        ident = sb("ident", [128, 128])
        ident_bf = sb("ident_bf", [128, 128], BF16)
        ident_r = sb("ident_r", [128, 128], F32R)
        mask = sb("mask", [128, 2, 2, 32], BF16)
        pos_raw = sb("pos_raw", [H, S])
        pos_parts = sb("pos_parts", [H, 2, S], F32R)
        tiles_raw = sb("tiles_raw", [N_TILES, 2, S])
        tiles_r = sb("tiles_r", [N_TILES, 2, S], F32R)

        banks = [ctx.enter_context(nc.psum_tensor(f"bank{i}", [128, S], F32)) for i in range(8)]
        MX, SC, CTX = banks[0:2], banks[2:4], banks[4]
        X, Y, Z = banks[5:8]

        x_hidden = gate[:, :, :]
        parts2 = (x1T, oT)
        ring = (x_res[:, :, :], y[:, :, :], o_tok[:, :, :],
                xt_raw[:, :, :].rearrange("p a b -> p (a b)").rearrange("p (n e) -> p n e", n=NB))

        z_ring = [Pt[:, i, :].rearrange("p (n e) -> p n e", n=NB) for i in range(4)]
        h_ring = [c2[:, :, :], gate[:, 0:2, :]]

        x1_dram = nc.dram_tensor("x1_dram", [B, S, E], F32).ap()
        parts_dram = nc.dram_tensor("parts_dram", [2, 2, H // 2, 2, D, S], F32).ap()
        tok = "(n p) e -> p n e"

        win_in, weights_in, small_in, pos_in = sem("win_in"), sem("weights_in"), sem("small_in"), sem("pos_in")
        xt_in, xres_in, x1_out, x1_in = sem("xt_in"), sem("xres_in"), sem("x1_out"), [sem(f"x1_in{i}") for i in range(4)]
        parts_out = [[sem(f"{which}_parts_out{c}") for which in ("q", "k")] for c in range(2)]
        stacked = [sem(f"stacked{c}") for c in range(2)]
        maxrow = [sem(f"maxrow{g}") for g in range(QUADS)]
        posrow = sem("posrow")
        out_sem = [sem(f"out{i}") for i in range(4)]
        const_ready, const_step, mem_ready, v_ones, w_hi, w_lo, c_init = (
            sem(n) for n in ("const_ready", "const_step", "mem_ready", "v_ones", "w_hi", "w_lo", "c_init"))
        pos_split, pos_hi, c0_hi, c0_lo = sem("pos_split"), sem("pos_hi"), sem("c0_hi"), sem("c0_lo")
        waits_passed = sem("waits_passed")
        bias_ready = sem("bias_ready")
        mx_ready, sc_ready, mt_ready, pv_ready, ct_ready, v_ready, qk_ready, ot_ready, op_ready, xt_ready, f_ready = (
            sem(n) for n in ("mx_ready", "sc_ready", "mt_ready", "pv_ready", "ct_ready", "v_ready", "qk_ready",
                             "ot_ready", "op_ready", "xt_ready", "f_ready"))
        exp_done, ctx_done, maxrow_done, v_done, qkhi_done, othi_done, x1hi_done, gate_done, chi_done, xhi_done = (
            sem(n) for n in ("exp_done", "ctx_done", "maxrow_done", "v_done", "qkhi_done", "othi_done", "x1hi_done",
                             "gate_done", "chi_done", "xhi_done"))
        red_done, rden_done, o_done, qklo_done, otlo_done, y_done, stat_done, mv_done, x1_done = (
            sem(n) for n in ("red_done", "rden_done", "o_done", "qklo_done", "otlo_done", "y_done",
                             "stat_done", "mv_done", "x1_done"))
        x1lo_done, fc_done, c_done, clo_done, xlo_done = (
            sem(n) for n in ("x1lo_done", "fc_done", "c_done", "clo_done", "xlo_done"))
        masked_done, vareps_done, rstd_done = sem("masked_done"), sem("vareps_done"), sem("rstd_done")
        cu_ready, cu_sum, cuhi_done, culo_done = sem("cu_ready"), sem("cu_sum"), sem("cuhi_done"), sem("culo_done")
        t2_ready, t2hi, t2lo, o2_ready, h_done, z_done, st2, mv2, ve2, rs2, sh2, fin2 = (
            sem(n) for n in ("t2_ready", "t2hi", "t2lo", "o2_ready", "h_done", "z_done", "st2", "mv2", "ve2", "rs2", "sh2", "fin2"))

        block = ctx.enter_context(nc.Block())

        w_stage = Pt[:, :, :].rearrange("p a b -> p (a b)")
        STAGED = ((Win, w_stage[:, 0:1536]), (Wout, w_stage[:, 1536:2048]), (Wg, w_stage[:, 2048:3584]),
                  (Wo, w_stage[:, 3584:4096]), (Ug, gate[:, :, :].rearrange("p a b -> p (a b)")), (Uo, ctx_raw[:, :]))

        own_wait = (nc.gpsimd.engine, nc.sync.engine)

        def real(t):
            return not isinstance(t, int) or 0 <= t < B

        def wait(eng, s, per, t, k):
            if isinstance(t, int):
                if t < 0:
                    return
                k, t = (per, B - 1) if t >= B else (k, t)
                if per * t + k <= 0:
                    return
            eng.wait_ge(s, per * t + k)
            if not isinstance(t, int) and eng.engine in own_wait:
                stand_alone(eng)

        def stand_alone(eng):
            eng.sem_inc(waits_passed, 1)

        def before(t, g):
            return (t, g - 1) if g else (t - 1, QUADS - 1)

        def freed(eng, t, *users):
            for s, per, dt, k in (users if isinstance(t, int) else users[:1]):
                wait(eng, s, per, t + dt, k)

        LAST_GATES = (*MX, *SC, CTX)

        def gate_bank(t, k, bank):
            return LAST_GATES[k] if isinstance(t, int) and t == B - 1 and k < len(LAST_GATES) else bank

        def head(g, hh):
            h = 4 * g + hh
            return 64 * (h % 2), h // 2

        def steps(eng, step, last=B):
            for t in range(PEELED):
                step(t, t // 4, t % 4)
            rounds = (last - PEELED) // 4
            with eng.Fori(0, rounds) as r:
                for i in range(PEELED, PEELED + 4):
                    step(4 * r + i, r + i // 4, i % 4)
            for t in range(4 * rounds + PEELED, B):
                step(t, t // 4, t % 4)

        @block.sync
        def _(sp):
            v = "(c p) n -> p c n"
            sp.dma_start(xt_raw[:, :, :], xt[0].rearrange("(c p) s -> p c s", p=128)).then_inc(xt_in, 16)
            sp.dma_start(w_stage[:, 0:1536].rearrange("p (c n) -> p c n", c=KC), w_in.rearrange(v, p=128)).then_inc(win_in, 16)
            sp.dma_start(pos_raw[:, :], pos_bias).then_inc(pos_in, 16)
            sp.dma_start(tiles_raw[:, :, :], tile_rows).then_inc(pos_in, 16)
            sp.dma_start(bias_raw[:, :, :], b_gates).then_inc(small_in, 16)
            sp.dma_start(inc_sb[:, :], in_c).then_inc(small_in, 16)
            sp.dma_start(bo_sb[:, :], b_o).then_inc(small_in, 16)
            sp.dma_start(w_stage[:, 1536:2048].rearrange("p (c n) -> p c n", c=KC), w_out.rearrange(v, p=128)).then_inc(weights_in, 16)
            sp.dma_start(w_stage[:, 2048:3584].rearrange("p (c n) -> p c n", c=KC), w_gates.rearrange(v, p=128)).then_inc(weights_in, 16)
            sp.dma_start(w_stage[:, 3584:4096].rearrange("p (c n) -> p c n", c=KC), w_o.rearrange(v, p=128)).then_inc(weights_in, 16)
            sp.dma_start(gate[:, :, :].rearrange("p a b -> p (a b)").rearrange("p (c n) -> p c n", c=KC),
                         u_gates.rearrange(v, p=128)).then_inc(weights_in, 16)
            sp.dma_start(ctx_raw[:, :].rearrange("p (c n) -> p c n", c=KC), u_o.rearrange(v, p=128)).then_inc(weights_in, 16)

            def constant_rows():
                sp.wait_ge(pos_split, 2)
                for par in range(2):
                    r = 64 * par + ROW_TILE
                    for which, dst in enumerate((Qs, Ks)):
                        sp.dma_start(dst[r:r + N_TILES, :, :].bitcast(F32),
                                     tiles_r[:, which, :].bitcast(F32).unsqueeze(1).to_broadcast([N_TILES, H // 2, S])).then_inc(posrow, 16)
                    for part in range(2):
                        r = 64 * par + ROW_BIAS + part
                        sp.dma_start(Ks[r:r + 1, :, :].bitcast(F32),
                                     pos_parts[H // 2 * par:H // 2 * (par + 1), part, :].bitcast(F32)).then_inc(posrow, 16)

            def parts_to_dram(t, c):
                wait(sp, stacked[c], 16 * STACK_DMAS, t - 1, 16 * STACK_DMAS)
                for which in range(2):
                    wait(sp, qklo_done, 4, t, 2 * c + which + 1)
                    for part in range(2):
                        sp.dma_start(parts_dram[c, which, :, part, :, :],
                                     qk_parts[:, c, which, part, :].bitcast(F32)).then_inc(parts_out[c][which], 16)

            def stack(t, c):
                wait(sp, sc_ready, 32, t - 1, 16 * c + 16)
                for which in range(2):
                    wait(sp, parts_out[c][which], 32, t, 32)
                for which, (dst, groups) in enumerate(((Qs, ROWS_Q), (Ks, ROWS_K))):
                    src = parts_dram[c, which].rearrange("(b o) l d s -> o (l d) b s", o=2)
                    for odd in range(2):
                        for r, part, n in groups:
                            sp.dma_start(dst[64 * odd + r:64 * odd + r + n * D, 4 * c:4 * c + 4, :].bitcast(F32),
                                         src[odd, part * D:(part + n) * D, :, :]).then_inc(stacked[c], 16)

            def max_to_stack(t, g):
                wait(sp, maxrow_done, 4, t, g + 1)
                for odd in range(2):
                    r = 64 * odd + ROW_MAX
                    sp.dma_start(Qs[r:r + 1, 2 * g:2 * g + 2, :].bitcast(F32),
                                 max_rows[8 * odd:8 * odd + 8, :].bitcast(F32)).then_inc(maxrow[g], 16)

            def iteration(t):
                if real(t + 1):
                    wait(sp, xlo_done, 2, t, 2)
                    sp.dma_start(xt_raw[:, :, :], xt[t + 1].rearrange("(c p) s -> p c s", p=128)).then_inc(xt_in, 16)
                if real(t - 1):
                    wait(sp, y_done, 2, t - 2, 2)
                    sp.dma_start(x_res[:, :, :], x[t - 1].rearrange(tok, p=128)).then_inc(xres_in, 16)
                if real(t):
                    max_to_stack(t, 0)
                    parts_to_dram(t, 1)
                    stack(t, 1)
                    max_to_stack(t, 1)
                if real(t - 1):
                    wait(sp, x1_done, 4, t - 1, 4)
                    sp.dma_start(x1_dram[t - 1].rearrange(tok, p=128), y[:, :, :]).then_inc(x1_out, 16)
                if real(t):
                    if real(t + 1):
                        parts_to_dram(t + 1, 0)
                    max_to_stack(t, 2)
                    if real(t + 1):
                        stack(t + 1, 0)
                    max_to_stack(t, 3)

            sp.wait_ge(mem_ready, 2)
            constant_rows()
            parts_to_dram(0, 0)
            stack(0, 0)
            iteration(0)
            iteration(1)
            with sp.Fori(2, B - 1) as t:
                iteration(t)
            iteration(B - 1)
            iteration(B)
            iteration(B + 1)

            sp.wait_ge(x1_out, 16 * B)
            sp.wait_ge(xt_ready, 2 * B)
            def load(t, i):
                sp.dma_start(ring[i], x1_dram[t].rearrange(tok, p=128)).then_inc(x1_in[i], 16)

            def move(t, rnd, i):
                if not isinstance(t, int) or t + 4 < B:
                    sp.wait_ge(z_done, t + 1)
                    stand_alone(sp)
                    load(t + 4, i)
                sp.wait_ge(fin2, 4 * t + 4)
                stand_alone(sp)
                sp.dma_start(out[t].rearrange(tok, p=128), z_ring[i]).then_inc(out_sem[i], 16)

            for i in range(4):
                load(i, i)
            steps(sp, move, B - 4)
            for i in range(4):
                sp.wait_ge(out_sem[i], 16 * B // 4)

        @block.gpsimd
        def _(pool):
            gp = nc.gpsimd
            gp.memset(Qs[:, :, :].bitcast(F32), 1.0).then_inc(mem_ready, 1)
            gp.memset(ident[:, :], 0.0).then_inc(const_step, 1)
            gp.memset(mask[:, :, :, :], 0.0).then_inc(const_step, 1)
            gp.memset(minus_half[:, :], -0.5).then_inc(const_step, 1)
            pool.wait_ge(const_step, 3)
            gp.affine_select(out=ident[:, :], in_=ident[:, :], compare_op=ALU.not_equal, fill=1.0, base=0,
                             pattern=[[-1, 128]], channel_multiplier=1).then_inc(const_step, 1)
            gp.memset(mask[:, 0, 0, :], MASKED).then_inc(const_step, 1)
            for m in range(4):
                own, prev = mask[32 * m:32 * m + 32, :, 1, :], mask[32 * m:32 * m + 32, 1, 0, :]
                pool.wait_ge(const_step, 5 + 2 * m)
                gp.affine_select(out=own, in_=own, compare_op=ALU.is_ge, fill=MASKED, base=0,
                                 pattern=[[0, 2], [-1, 32]], channel_multiplier=1).then_inc(const_step, 1)
                pool.wait_ge(const_step, 6 + 2 * m)
                gp.affine_select(out=prev, in_=prev, compare_op=ALU.is_ge, fill=MASKED, base=0,
                                 pattern=[[1, 32]], channel_multiplier=-1).then_inc(const_step, 1)
            pool.wait_ge(const_step, 13)
            gp.tensor_copy(ident_bf[:, :], ident[:, :]).then_inc(const_ready, 1)
            gp.tensor_copy(ident_r[:, :], ident[:, :]).then_inc(const_ready, 1)
            gp.memset(Vp[:, :, :], 1.0).then_inc(v_ones, 1)

            def window(t, g, hh):
                p4 = Pt[:, hh, :].rearrange("p (j c) -> p j c", c=256)
                wait(pool, exp_done, 32, t, 8 * g + 2 * hh + 2)
                gp.affine_select(out=p4[:, :, 0:128], in_=p4[:, :, 0:128], compare_op=ALU.is_ge, fill=0.0, base=0,
                                 pattern=[[0, 4], [1, 128]], channel_multiplier=-1)
                gp.affine_select(out=p4[:, 0:3, 128:256], in_=p4[:, 0:3, 128:256], compare_op=ALU.is_ge, fill=0.0, base=0,
                                 pattern=[[0, 3], [-1, 128]], channel_multiplier=1).then_inc(masked_done, 1)

            def inverse_std(t):
                wait(pool, mv_done, 4, t, 4)
                gp.tensor_scalar(var_eps[:, :], mean_var[:, 0, :, 1], EPS, None, ALU.add).then_inc(vareps_done, 1)
                wait(pool, vareps_done, 1, t, 1)
                wait(pool, x1_done, 4, t - 1, 4)
                gp.tensor_tensor(rstd[:, 0, :], var_eps[:, :], minus_half[:, :], ALU.pow).then_inc(rstd_done, 1)

            def iteration(t):
                for g in range(QUADS):
                    pt, pg = before(t, g)
                    if real(pt):
                        for hh in range(4):
                            window(pt, pg, hh)
                    if g == 1 and real(t - 1):
                        inverse_std(t - 1)

            iteration(0)
            iteration(1)
            with pool.Fori(2, B - 1) as t:
                iteration(t)
            iteration(B - 1)
            iteration(B)

            def second(t, rnd, i):
                if not isinstance(t, int) or t >= 2:
                    pool.wait_ge(fin2, 4 * t - 4)
                    stand_alone(pool)
                pool.wait_ge(mv2, 4 * t + 4)
                stand_alone(pool)
                if not isinstance(t, int) or t >= 1:
                    pool.wait_ge(sh2, t)
                    stand_alone(pool)
                gp.tensor_scalar(var_eps[:, :], mean_var[:, i % 2, :, 1], EPS, None, ALU.add).then_inc(ve2, 1)
                gp.tensor_scalar(minus_mean[:, :], mean_var[:, i % 2, :, 0], -1.0, None, ALU.mult).then_inc(ve2, 1)
                pool.wait_ge(ve2, 2 * t + 2)
                stand_alone(pool)
                gp.tensor_tensor(rstd[:, i % 2, :], var_eps[:, :], minus_half[:, :], ALU.pow).then_inc(rs2, 1)
                pool.wait_ge(rs2, t + 1)
                stand_alone(pool)
                gp.tensor_tensor(shift[:, i % 2, :], minus_mean[:, :], rstd[:, i % 2, :], ALU.mult).then_inc(sh2, 1)

            steps(pool, second)

        @block.scalar
        def _(act):
            sc = nc.scalar

            def weights_hi(n):
                dst, src = STAGED[n]
                sc.activation(dst[:, 0, :, :].rearrange("p a b -> p (a b)"), src, ACT.Copy).then_inc(w_hi, 1)

            def x_hi(t, c):
                if c == 0:
                    wait(act, xt_in, 16, t, 16)
                    wait(act, v_ready, 2, t - 1, 2)
                sc.activation(xT[:, 0, c, :], xt_raw[:, c, :], ACT.Copy).then_inc(xhi_done, 1)

            def qk_hi(t, k, bank):
                wait(act, parts_out[k // 2][k % 2], 32, t - 1, 32)
                wait(act, qk_ready, 4, t, k + 1)
                sc.activation(qk_parts[:, k // 2, k % 2, 0, :], bank[:, :], ACT.Copy,
                              scale=float(D) ** -0.5 if k % 2 == 0 else 1.0).then_inc(qkhi_done, 1)

            def v_out(t, half, bank):
                if half == 0:
                    wait(act, pv_ready, 4, t - 1, 4)
                wait(act, v_ready, 2, t, half + 1)
                sc.activation(Vp[:, 2 * half:2 * half + 2, 0:H * PITCH].rearrange("p n (h d) -> p n h d", d=PITCH)[:, :, :, 0:D],
                              bank[:, :].rearrange("p (n h d) -> p n h d", n=2, h=H), ACT.Copy).then_inc(v_done, 1)

            def exps(t, g, hh):
                if hh == 0:
                    wait(act, pv_ready, 4, t, g)
                for a, n in enumerate((S, S - WIN)):
                    wait(act, sc_ready, 32, t, 8 * g + 2 * hh + a + 1)
                    sc.activation(Pt[:, hh, S * a:S * a + n], SC[a][:, 0:n], ACT.Exp).then_inc(exp_done, 1)

            def max_row(t, g):
                pt, pg = before(t, g)
                wait(act, maxrow[pg], 16 * MAXROW_DMAS, pt, 16 * MAXROW_DMAS)
                wait(act, mt_ready, 4, t, g + 1)
                sc.activation(max_rows[:, :], CTX[0:16, 0:128], ACT.Copy, scale=-1.0).then_inc(maxrow_done, 1)

            def ctx_out(t, g):
                wait(act, pv_ready, 4, t, g + 1)
                wait(act, ct_ready, 4, t, g)
                sc.activation(ctx_raw[:, :], CTX[:, :], ACT.Copy).then_inc(ctx_done, 1)

            def ot_hi(t, c, bank):
                if c == 0:
                    wait(act, op_ready, 2, t - 1, 2)
                wait(act, ot_ready, 2, t, c + 1)
                sc.activation(oT[:, 0, c, :], bank[:, :], ACT.Copy).then_inc(othi_done, 1)

            def x1_hi(t, c, bank):
                if c == 0:
                    wait(act, f_ready, 6, t - 1, 6)
                wait(act, xt_ready, 2, t, c + 1)
                sc.activation(x1T[:, 0, c, :], bank[:, :], ACT.Copy).then_inc(x1hi_done, 1)

            def gates(t, k, bank):
                j, which = k // 3, k % 3
                wait(act, c_done, 2, t, j)
                wait(act, f_ready, 6, t, k + 1)
                bank = gate_bank(t, k, bank)
                if which < 2:
                    ins = sc.activation(gate[:, which, :], bank[:, :], ACT.Tanh, bias=bias_half[:, which, j:j + 1], scale=0.5)
                else:
                    ins = sc.activation(gate[:, which, :], bank[:, :], ACT.Tanh, bias=bias_raw[:, which, j:j + 1])
                ins.then_inc(gate_done, 1)

            def c_hi(t):
                wait(act, f_ready, 6, t, 6)
                for j in range(KC):
                    wait(act, c_done, 2, t, j + 1)
                    sc.activation(cT[:, 0, j, :], c2[:, j, :], ACT.Copy, scale=0.5).then_inc(chi_done, 1)

            def iteration(t):
                p1, p2, n1, now = real(t - 1), real(t - 2), real(t + 1), real(t)
                if p1: exps(t - 1, 3, 0)
                if p2: gates(t - 2, 4, Y)
                if p1: exps(t - 1, 3, 1)
                if p2: gates(t - 2, 5, Z)
                if p1: exps(t - 1, 3, 2)
                if now: qk_hi(t, 2, X)
                if p1: exps(t - 1, 3, 3)
                if now: max_row(t, 0)
                if now: qk_hi(t, 3, Y)
                if p1: ctx_out(t - 1, 3)
                if p2: c_hi(t - 2)

                if now: exps(t, 0, 0)
                if now: v_out(t, 0, X)
                if now: exps(t, 0, 1)
                if p1:
                    ot_hi(t - 1, 0, Z)
                    ot_hi(t - 1, 1, X)
                if now: exps(t, 0, 2)
                if now: v_out(t, 1, Y)
                if n1: x_hi(t + 1, 0)
                if now: exps(t, 0, 3)
                if n1: x_hi(t + 1, 1)
                if now: max_row(t, 1)
                if now: ctx_out(t, 0)

                if now: exps(t, 1, 0)
                if now: exps(t, 1, 1)
                if n1: qk_hi(t + 1, 0, Z)
                if now: exps(t, 1, 2)
                if p1:
                    x1_hi(t - 1, 0, Y)
                    x1_hi(t - 1, 1, Z)
                if now: exps(t, 1, 3)
                if n1: qk_hi(t + 1, 1, X)
                if now: max_row(t, 2)
                if p1: gates(t - 1, 0, Y)
                if now: ctx_out(t, 1)

                if now: exps(t, 2, 0)
                if now: exps(t, 2, 1)
                if p1: gates(t - 1, 1, X)
                if now: exps(t, 2, 2)
                if p1: gates(t - 1, 2, Y)
                if now: exps(t, 2, 3)
                if now: max_row(t, 3)
                if now: ctx_out(t, 2)
                if p1: gates(t - 1, 3, X)

            def last_sequence():
                t = B - 1
                for hh in range(4):
                    exps(t, QUADS - 1, hh)
                gates(t - 1, 4, Y)
                ctx_out(t, 3)
                gates(t - 1, 5, X)
                ot_hi(t, 0, Z)
                ot_hi(t, 1, X)
                c_hi(t - 1)
                x1_hi(t, 0, Y)
                x1_hi(t, 1, Z)
                for k in range(4):
                    gates(t, k, None)

            for c in range(KC):
                x_hi(0, c)
            act.wait_ge(win_in, 16)
            weights_hi(0)
            act.wait_ge(pos_in, 32)
            sc.activation(tiles_r[:, :, :], tiles_raw[:, :, :], ACT.Copy).then_inc(pos_split, 1)
            sc.activation(pos_parts[:, 0, :], pos_raw[:, :], ACT.Copy).then_inc(pos_hi, 1)
            qk_hi(0, 0, Z)
            qk_hi(0, 1, X)
            act.wait_ge(weights_in, 80)
            for n in range(1, 6):
                weights_hi(n)
            act.wait_ge(bias_ready, 1)
            act.wait_ge(c_init, 2)
            for j in range(KC):
                sc.activation(cT[:, 0, j, :], c2[:, j, :], ACT.Copy, scale=0.5).then_inc(c0_hi, 1)
            act.wait_ge(v_ones, 1)
            act.wait_ge(w_lo, 6)
            iteration(0)
            iteration(1)
            with act.Fori(2, B - 1) as t:
                iteration(t)
            iteration(B - 1)
            last_sequence()
            iteration(B + 1)

            def hi2(t, i):
                if not isinstance(t, int) or t >= 2:
                    act.wait_ge(o2_ready, 2 * t - 2)
                for c in range(KC):
                    act.wait_ge(t2_ready, 2 * t + (c + 1))
                    sc.activation(parts2[i][:, 0, c, :], banks[2 * i + c][:, :], ACT.Copy).then_inc(t2hi, 1)

            def hidden(t, rnd, i):
                if not isinstance(t, int) or 1 < t + 1 < B:
                    hi2(t + 1, (i + 1) % 2)
                if not isinstance(t, int) or t >= 2:
                    act.wait_ge(z_done, t - 1)
                for a in range(2):
                    act.wait_ge(o2_ready, 2 * t + (a + 1))
                    sc.activation(h_ring[i % 2][:, a, :], banks[4 + 2 * (i % 2) + a][:, :], ACT.Tanh).then_inc(h_done, 1)
                if not isinstance(t, int) or t >= 1:
                    layernorm2(t - 1, i - 1)

            def layernorm2(t, i):
                act.wait_ge(sh2, t + 1)
                z = z_ring[i % 4]
                for n in range(NB):
                    sc.activation(z[:, n, :], z[:, n, :], ACT.Identity, bias=shift[:, i % 2, n:n + 1],
                                  scale=rstd[:, i % 2, n:n + 1]).then_inc(fin2, 1)

            hi2(0, 0)
            hi2(1, 1)
            for a in range(2):
                act.wait_ge(cu_sum, a + 1)
                sc.activation(cu[:, 0, 2 * a:2 * a + 2, :], x_hidden[:, a, :].rearrange("p (n e) -> p n e", n=2), ACT.Copy).then_inc(cuhi_done, 1)
            steps(act, hidden)
            layernorm2(B - 1, B - 1)

        @block.vector
        def _(dve):
            ve = nc.vector

            def minus_hi(out_, in_, hi, scale=1.0):
                return ve.scalar_tensor_tensor(out_, in_, scale, hi.bitcast(F32), op0=ALU.mult, op1=ALU.subtract)


            def weights_lo(n):
                dst, src = STAGED[n]
                dve.wait_ge(w_hi, n + 1)
                minus_hi(dst[:, 1, :, :].rearrange("p a b -> p (a b)"), src,
                         dst[:, 0, :, :].rearrange("p a b -> p (a b)")).then_inc(w_lo, 1)

            def x_lo(t, c):
                wait(dve, xhi_done, 2, t, c + 1)
                minus_hi(xT[:, 1, c, :], xt_raw[:, c, :], xT[:, 0, c, :]).then_inc(xlo_done, 1)

            def qk_lo(t, k, bank):
                wait(dve, qkhi_done, 4, t, k + 1)
                minus_hi(qk_parts[:, k // 2, k % 2, 1, :], bank[:, :], qk_parts[:, k // 2, k % 2, 0, :],
                         float(D) ** -0.5 if k % 2 == 0 else 1.0).then_inc(qklo_done, 1)

            def maxima(t, g, hh):
                if hh == 0:
                    wait(dve, mt_ready, 4, t, g)
                for a in range(2):
                    wait(dve, mx_ready, 32, t, 8 * g + 2 * hh + a + 1)
                    at = 8 * (hh % 2) + 4 * (hh // 2) + 2 * a
                    ve.tensor_reduce(out=max_q[:, at:at + 2],
                                     in_=MX[a][:, :].rearrange("p (n k) -> p n k", n=2), axis=AX.X, op=ALU.max).then_inc(red_done, 1)

            def normalise(t, g, bank):
                c4 = bank[:, :].rearrange("p (n h d) -> p n h d", n=NB, h=4)
                wait(dve, ct_ready, 4, t, g + 1)
                wait(dve, o_done, 4, t, g)
                ve.reciprocal(rden[:, :].rearrange("p (n h) -> p n h", n=NB), c4[:, :, :, D]).then_inc(rden_done, 1)
                wait(dve, rden_done, 4, t, g + 1)
                wait(dve, ot_ready, 2, t - 1, 2)
                o4 = o_tok[:, :, 4 * D * g:4 * D * (g + 1)].rearrange("p n (h d) -> p n h d", h=4)
                r4 = rden[:, :].rearrange("p (n h) -> p n h", n=NB).unsqueeze(3).to_broadcast([128, NB, 4, D])
                ve.tensor_tensor(o4, c4[:, :, :, 0:D], r4, ALU.mult).then_inc(o_done, 1)

            def ot_lo(t, c, bank):
                wait(dve, othi_done, 2, t, c + 1)
                minus_hi(oT[:, 1, c, :], bank[:, :], oT[:, 0, c, :]).then_inc(otlo_done, 1)

            def residual(t, half, bank):
                if half == 0:
                    wait(dve, xres_in, 16, t, 16)
                    wait(dve, xt_ready, 2, t - 1, 2)
                    wait(dve, x1_out, 16, t - 1, 16)
                wait(dve, op_ready, 2, t, half + 1)
                ve.tensor_tensor(y[:, 2 * half:2 * half + 2, :], bank[:, :].rearrange("p (n e) -> p n e", n=2),
                                 x_res[:, 2 * half:2 * half + 2, :], ALU.add).then_inc(y_done, 1)

            def statistics(t):
                for n in range(NB):
                    wait(dve, y_done, 2, t, n // 2 + 1)
                    ve.bn_stats(stats[:, n, :], y[:, n, :]).then_inc(stat_done, 1)
                for n in range(NB):
                    wait(dve, stat_done, 4, t, n + 1)
                    stand_alone(dve)
                    ve.bn_aggr(mean_var[:, 0, n, :], stats[:, n, :]).then_inc(mv_done, 1)

            def layernorm(t):
                wait(dve, rstd_done, 1, t, 1)
                for n in range(NB):
                    ve.tensor_scalar(y[:, n, :], y[:, n, :], mean_var[:, 0, n, 0:1], rstd[:, 0, n:n + 1],
                                     ALU.subtract, ALU.mult).then_inc(x1_done, 1)

            def x1_lo(t, c, bank):
                wait(dve, x1hi_done, 2, t, c + 1)
                minus_hi(x1T[:, 1, c, :], bank[:, :], x1T[:, 0, c, :]).then_inc(x1lo_done, 1)

            def update(t, j):
                wait(dve, gate_done, 6, t, 3 * j + 1)
                if j == 0:
                    wait(dve, chi_done, 2, t - 1, 2)
                ve.scalar_tensor_tensor(gate[:, 0, :], gate[:, 0, :], 1.0, c2[:, j, :], op0=ALU.add, op1=ALU.mult).then_inc(fc_done, 1)
                wait(dve, gate_done, 6, t, 3 * j + 3)
                ve.scalar_tensor_tensor(gate[:, 1, :], gate[:, 1, :], 1.0, gate[:, 2, :], op0=ALU.add, op1=ALU.mult).then_inc(fc_done, 1)
                wait(dve, fc_done, 4, t, 2 * j + 2)
                ve.scalar_tensor_tensor(c2[:, j, :], gate[:, 0, :], 0.5, gate[:, 1, :], op0=ALU.mult, op1=ALU.add).then_inc(c_done, 1)

            def c_lo(t):
                for j in range(KC):
                    wait(dve, chi_done, 2, t, j + 1)
                    minus_hi(cT[:, 1, j, :], c2[:, j, :], cT[:, 0, j, :], 0.5).then_inc(clo_done, 1)

            def iteration(t):
                p1, p2, n1, now = real(t - 1), real(t - 2), real(t + 1), real(t)
                if now:
                    for hh in range(4):
                        maxima(t, 0, hh)
                if p1: normalise(t - 1, 2, Z)
                if now: qk_lo(t, 2, X)
                if p2: update(t - 2, 1)
                if now: qk_lo(t, 3, Y)

                if now: maxima(t, 1, 0)
                if p1: normalise(t - 1, 3, Z)
                if p2: c_lo(t - 2)
                if now: maxima(t, 1, 1)
                if p1:
                    ot_lo(t - 1, 0, Z)
                    ot_lo(t - 1, 1, X)
                if now: maxima(t, 1, 2)
                if now: maxima(t, 1, 3)
                if n1: x_lo(t + 1, 0)
                if p1: residual(t - 1, 0, Z)
                if n1: x_lo(t + 1, 1)
                if p1: residual(t - 1, 1, X)
                if p1: statistics(t - 1)

                if now: maxima(t, 2, 0)
                if now: normalise(t, 0, Y)
                if now: maxima(t, 2, 1)
                if p1: layernorm(t - 1)
                if n1: qk_lo(t + 1, 0, Z)
                if now: maxima(t, 2, 2)
                if p1:
                    x1_lo(t - 1, 0, Y)
                    x1_lo(t - 1, 1, Z)
                if now: maxima(t, 2, 3)
                if n1: qk_lo(t + 1, 1, X)

                if now:
                    for hh in range(4):
                        maxima(t, 3, hh)
                    normalise(t, 1, Z)
                if p1: update(t - 1, 0)

            def last_sequence():
                t = B - 1
                normalise(t, 2, Z)
                normalise(t, 3, Z)
                ot_lo(t, 0, Z)
                ot_lo(t, 1, X)
                update(t - 1, 1)
                residual(t, 0, Z)
                c_lo(t - 1)
                residual(t, 1, X)
                statistics(t)
                layernorm(t)
                x1_lo(t, 0, Y)
                x1_lo(t, 1, Z)
                update(t, 0)

            ve.memset(c2[:, :, :], 2.0).then_inc(c_init, 1)
            ve.memset(Ks[:, :, :].bitcast(F32), 1.0).then_inc(mem_ready, 1)
            for c in range(KC):
                x_lo(0, c)
            weights_lo(0)
            dve.wait_ge(pos_hi, 1)
            minus_hi(pos_parts[:, 1, :], pos_raw[:, :], pos_parts[:, 0, :]).then_inc(pos_split, 1)
            qk_lo(0, 0, Z)
            qk_lo(0, 1, X)
            dve.wait_ge(small_in, 48)
            ve.tensor_scalar(bias_half[:, :, :], bias_raw[:, 0:2, :], 0.5, None, ALU.mult).then_inc(bias_ready, 1)
            dve.wait_ge(c_init, 1)
            for j in range(KC):
                ins = ve.tensor_scalar(c2[:, j, :], c2[:, j, :], inc_sb[:, j:j + 1], None, ALU.mult)
            ins.then_inc(c_init, 1)
            for n in range(1, 6):
                weights_lo(n)
            for j in range(KC):
                dve.wait_ge(c0_hi, j + 1)
                minus_hi(cT[:, 1, j, :], c2[:, j, :], cT[:, 0, j, :], 0.5).then_inc(c0_lo, 1)
            iteration(0)
            iteration(1)
            with dve.Fori(2, B - 1) as t:
                iteration(t)
            iteration(B - 1)
            last_sequence()
            iteration(B + 1)

            def lo2(t, i):
                for c in range(KC):
                    dve.wait_ge(t2hi, 2 * t + (c + 1))
                    minus_hi(parts2[i][:, 1, c, :], banks[2 * i + c][:, :], parts2[i][:, 0, c, :]).then_inc(t2lo, 1)

            def finish(t, rnd, i):
                if not isinstance(t, int) or 1 < t + 1 < B:
                    lo2(t + 1, (i + 1) % 2)
                if not isinstance(t, int) or t >= 4:
                    dve.wait_ge(out_sem[i], 16 * rnd)
                dve.wait_ge(h_done, 2 * t + 2)
                ve.tensor_tensor(z_ring[i], h_ring[i % 2].rearrange("p a (n e) -> p (a n) e", e=E), ring[i], ALU.add).then_inc(z_done, 1)
                dve.wait_ge(z_done, t + 1)
                for n in range(NB):
                    ve.bn_stats(stats[:, n, :], z_ring[i][:, n, :]).then_inc(st2, 1)
                if not isinstance(t, int) or t >= 2:
                    dve.wait_ge(sh2, t - 1)
                    stand_alone(dve)
                for n in range(NB):
                    dve.wait_ge(st2, 4 * t + (n + 1))
                    stand_alone(dve)
                    ve.bn_aggr(mean_var[:, i % 2, n, :], stats[:, n, :]).then_inc(mv2, 1)

            lo2(0, 0)
            lo2(1, 1)
            for a in range(2):
                dve.wait_ge(cu_ready, a + 1)
                ve.tensor_tensor(x_hidden[:, a, :].rearrange("p (n e) -> p n e", n=2), banks[6 + a][:, :].rearrange("p (n e) -> p n e", n=2),
                                 bo_sb[:, :].unsqueeze(1).to_broadcast([128, 2, E]), ALU.add).then_inc(cu_sum, 1)
            for a in range(2):
                dve.wait_ge(cuhi_done, a + 1)
                minus_hi(cu[:, 1, 2 * a:2 * a + 2, :], x_hidden[:, a, :].rearrange("p (n e) -> p n e", n=2),
                         cu[:, 0, 2 * a:2 * a + 2, :]).then_inc(culo_done, 1)
            steps(dve, finish)

        @block.tensor
        def _(pe):
            te = nc.tensor
            TOGETHER = ((0, 0), (0, 1), (0, 2), (1, 0), (1, 1), (2, 2), (3, 2))
            PASSES = ((0, 0), (0, 1), (1, 0))

            def product(out_, pairs, s, first=True, last=True):
                todo = [(w(a), m(b)) for w, m in pairs for a, b in PASSES]
                for n, (w, m) in enumerate(todo):
                    ins = te.matmul(out_, w, m, start=(first and n == 0), stop=(last and n == len(todo) - 1))
                if s is not None:
                    ins.then_inc(s, 1)

            def masked_scores(t, g, hh):
                base, blk = head(g, hh)
                if hh == 0:
                    wait(pe, stacked[g // 2], 16 * STACK_DMAS, t, 16 * STACK_DMAS)
                q, k = Qs[base:base + K_MAXIMA, blk, :], Ks[base:base + K_MAXIMA, blk, :]
                for halves in ((0, 1),) if (g, hh) in TOGETHER else ((0,), (1,)):
                    for a in halves:
                        wait(pe, red_done, 32, t, 8 * g + 2 * hh + a - 1)
                        for n in (2 * a, 2 * a + 1):
                            keys = k[:, (n - 1) * WIN:(n + 1) * WIN] if n else k[:, 0:WIN].unsqueeze(1).to_broadcast([K_MAXIMA, 2, WIN])
                            te.matmul(MX[a][:, 256 * (n % 2):256 * (n % 2) + 256], q[:, n * WIN:(n + 1) * WIN], keys,
                                      start=(n % 2 == 0), stop=False, skip_group_check=True)
                    for a in halves:
                        for m in range(4):
                            cut = MX[a][32 * m:32 * m + 32, :].rearrange("p (n c) -> p n c", n=4)[:, :, 32 * m:32 * m + 32]
                            edge = mask[:, :, :, :].rearrange("p n b c -> p (n b) c") if a == 0 else \
                                mask[:, 1, :, :].unsqueeze(1).to_broadcast([128, 2, 2, 32])
                            ins = te.matmul(cut, ident_bf[:, 32 * m:32 * m + 32], edge, start=False, stop=True, skip_group_check=True)
                        ins.then_inc(mx_ready, 1)

            def max_transpose(t, g):
                wait(pe, red_done, 32, t, 8 * g + 8)
                wait(pe, ctx_done, 4, t, g - 1)
                te.transpose(CTX[0:16, 0:128], max_q[:, :], ident[:, :]).then_inc(mt_ready, 1)

            def scores(t, g, hh):
                base, blk = head(g, hh)
                if hh == 0:
                    wait(pe, maxrow[g], 16 * MAXROW_DMAS, t, 16 * MAXROW_DMAS)
                q, k = Qs[base:base + K_SCORES, blk, :], Ks[base:base + K_SCORES, blk, :]
                for a in range(2):
                    wait(pe, exp_done, 32, t, 8 * g + 2 * hh + a - 1)
                    for j in (2 * a, 2 * a + 1):
                        width = min(2 * WIN, S - j * WIN)
                        ins = te.matmul(SC[a][:, 256 * (j % 2):256 * (j % 2) + width], k[:, j * WIN:(j + 1) * WIN],
                                        q[:, j * WIN:j * WIN + width], start=True, stop=True)
                    ins.then_inc(sc_ready, 1)

            def values(t, g, slot_t):
                wait(pe, masked_done, 16, t, 4 * g + 4)
                if g == 0:
                    wait(pe, v_done, 2, t, 2)
                nt, ng = (t, g + 1) if g < 3 else (slot_t, 0)
                if real(nt):
                    wait(pe, maxrow_done, 4, nt, ng + 1)
                else:
                    wait(pe, ctx_done, 4, t, g)
                for j in range(NB):
                    width = min(2 * WIN, S - j * WIN)
                    for hh in range(4):
                        h = 4 * g + hh
                        ins = te.matmul(CTX[32 * hh:32 * hh + 32, j * WIN:j * WIN + width], Vp[:, j, PITCH * h:PITCH * h + 32],
                                        Pt[:, hh, 256 * j:256 * j + width], start=(j == 0), stop=(j == NB - 1),
                                        skip_group_check=True)
                ins.then_inc(pv_ready, 1)

            def ctx_transpose(t, g, bank):
                wait(pe, ctx_done, 4, t, g + 1)
                for n in range(NB):
                    ins = te.transpose(bank[:, WIN * n:WIN * (n + 1)], ctx_raw[:, WIN * n:WIN * (n + 1)], ident[:, :])
                ins.then_inc(ct_ready, 1)

            def project_qk(t, k, bank):
                wait(pe, xlo_done, 2, t, 2)
                col = E * (k % 2) + 128 * (k // 2)
                product(bank[:, :], [(lambda a, c=c: Win[:, a, c, col:col + 128], lambda b, c=c: xT[:, b, c, :])
                                     for c in range(KC)], qk_ready)

            def project_v(t, half, bank):
                for n in (2 * half, 2 * half + 1):
                    product(bank[:, E * (n % 2):E * (n % 2) + E],
                            [(lambda a, c=c: xT[:, a, c, n * WIN:(n + 1) * WIN], lambda b, c=c: Win[:, b, c, 2 * E:3 * E])
                             for c in range(KC)], v_ready if n % 2 else None)

            def o_transpose(t, c, bank):
                wait(pe, o_done, 4, t, 4)
                for n in range(NB):
                    ins = te.transpose(bank[:, WIN * n:WIN * (n + 1)], o_tok[:, n, 128 * c:128 * c + 128], ident[:, :])
                ins.then_inc(ot_ready, 1)

            def project_out(t, half, bank):
                wait(pe, otlo_done, 2, t, 2)
                for n in (2 * half, 2 * half + 1):
                    product(bank[:, E * (n % 2):E * (n % 2) + E],
                            [(lambda a, c=c: oT[:, a, c, n * WIN:(n + 1) * WIN], lambda b, c=c: Wout[:, b, c, :])
                             for c in range(KC)], op_ready if n % 2 else None)

            def x1_transpose(t, c, bank):
                wait(pe, x1_done, 4, t, 4)
                for n in range(NB):
                    ins = te.transpose(bank[:, WIN * n:WIN * (n + 1)], y[:, n, 128 * c:128 * c + 128], ident[:, :])
                ins.then_inc(xt_ready, 1)

            def gate_pairs(k, weight, operand):
                col = E * (k % 3) + 128 * (k // 3)
                return [(lambda a, c=c: weight[:, a, c, col:col + 128], lambda b, c=c: operand[:, b, c, :]) for c in range(KC)]

            def last_gates_of_state(gates_of):
                pe.wait_ge(clo_done, 2 * (B - 1))
                pe.wait_ge(red_done, 32 * B)
                pe.wait_ge(exp_done, 32 * B)
                pe.wait_ge(ctx_done, 4 * B)
                for k in gates_of:
                    product(LAST_GATES[k][:, :], gate_pairs(k, Ug, cT), None, last=False)

            def gate_product(t, k, bank):
                if k == 0:
                    wait(pe, x1lo_done, 2, t, 2)
                    wait(pe, clo_done, 2, t - 1, 2)
                if gate_bank(t, k, bank) is bank:
                    product(bank[:, :], gate_pairs(k, Ug, cT) + gate_pairs(k, Wg, x1T), f_ready)
                else:
                    product(gate_bank(t, k, bank)[:, :], gate_pairs(k, Wg, x1T), f_ready, first=False)

            def iteration(t):
                p1, p2, n1, now = real(t - 1), real(t - 2), real(t + 1), real(t)

                def attend(g, hh):
                    pt, pg = before(t, g)
                    if now:
                        masked_scores(t, g, hh)
                    if real(pt):
                        scores(pt, pg, hh)

                attend(0, 0)
                if p2:
                    freed(pe, t, (gate_done, 6, -2, 3), (gate_done, 6, -2, 1), (x1lo_done, 2, -2, 1))
                    gate_product(t - 2, 4, Y)
                attend(0, 1)
                if p2:
                    freed(pe, t, (o_done, 4, -1, 2), (x1lo_done, 2, -2, 2), (qklo_done, 4, -1, 1))
                    gate_product(t - 2, 5, Z)
                attend(0, 2)
                if now:
                    freed(pe, t, (gate_done, 6, -2, 4), (gate_done, 6, -2, 2), (qklo_done, 4, 0, 2))
                    project_qk(t, 2, X)
                attend(0, 3)
                if p1:
                    freed(pe, t, (gate_done, 6, -2, 6), (o_done, 4, -1, 2), (x1lo_done, 2, -2, 2), (qklo_done, 4, 0, 1))
                    ctx_transpose(t - 1, 2, Z)
                if now:
                    max_transpose(t, 0)
                    freed(pe, t, (gate_done, 6, -2, 5), (gate_done, 6, -2, 3), (o_done, 4, -1, 1))
                    project_qk(t, 3, Y)
                if p1:
                    values(t - 1, 3, t)
                attend(1, 0)
                if p1:
                    freed(pe, t, (o_done, 4, -1, 3))
                    ctx_transpose(t - 1, 3, Z)
                if now:
                    freed(pe, t, (qklo_done, 4, 0, 3))
                    project_v(t, 0, X)
                attend(1, 1)
                if p1:
                    freed(pe, t, (o_done, 4, -1, 4))
                    o_transpose(t - 1, 0, Z)
                    freed(pe, t, (v_done, 2, 0, 1), (gate_done, 6, -2, 4), (qklo_done, 4, 0, 3))
                    o_transpose(t - 1, 1, X)
                attend(1, 2)
                if now:
                    freed(pe, t, (qklo_done, 4, 0, 4))
                    project_v(t, 1, Y)
                attend(1, 3)
                if p1:
                    freed(pe, t, (otlo_done, 2, -1, 1))
                    project_out(t - 1, 0, Z)
                if now:
                    max_transpose(t, 1)
                if p1:
                    freed(pe, t, (otlo_done, 2, -1, 2))
                    project_out(t - 1, 1, X)
                if now:
                    values(t, 0, t)
                attend(2, 0)
                if now:
                    freed(pe, t, (v_done, 2, 0, 2))
                    ctx_transpose(t, 0, Y)
                attend(2, 1)
                if n1:
                    freed(pe, t, (y_done, 2, -1, 1), (qklo_done, 4, 0, 1))
                    project_qk(t + 1, 0, Z)
                attend(2, 2)
                if p1:
                    freed(pe, t, (o_done, 4, 0, 1), (v_done, 2, 0, 2), (gate_done, 6, -2, 5))
                    x1_transpose(t - 1, 0, Y)
                    freed(pe, t, (qklo_done, 4, 1, 1), (y_done, 2, -1, 1))
                    x1_transpose(t - 1, 1, Z)
                attend(2, 3)
                if n1:
                    freed(pe, t, (y_done, 2, -1, 2), (v_done, 2, 0, 1))
                    project_qk(t + 1, 1, X)
                if now:
                    max_transpose(t, 2)
                if p1:
                    freed(pe, t, (x1lo_done, 2, -1, 1))
                    gate_product(t - 1, 0, Y)
                if now:
                    values(t, 1, t)
                attend(3, 0)
                attend(3, 1)
                if p1:
                    freed(pe, t, (qklo_done, 4, 1, 2), (y_done, 2, -1, 2))
                    gate_product(t - 1, 1, X)
                attend(3, 2)
                if p1:
                    freed(pe, t, (gate_done, 6, -1, 1))
                    gate_product(t - 1, 2, Y)
                attend(3, 3)
                if now:
                    freed(pe, t, (x1lo_done, 2, -1, 2), (qklo_done, 4, 1, 1))
                    ctx_transpose(t, 1, Z)
                    max_transpose(t, 3)
                if p1:
                    freed(pe, t, (gate_done, 6, -1, 2))
                    gate_product(t - 1, 3, X)
                if now:
                    values(t, 2, t)

            def last_sequence():
                t = B - 1
                for hh in range(4):
                    scores(t, QUADS - 1, hh)
                wait(pe, o_done, 4, t, 2)
                ctx_transpose(t, 2, Z)
                wait(pe, gate_done, 6, t - 1, 3)
                gate_product(t - 1, 4, Y)
                values(t, 3, B)
                wait(pe, gate_done, 6, t - 1, 4)
                gate_product(t - 1, 5, X)
                wait(pe, o_done, 4, t, 3)
                ctx_transpose(t, 3, Z)
                wait(pe, o_done, 4, t, 4)
                o_transpose(t, 0, Z)
                wait(pe, gate_done, 6, t - 1, 6)
                o_transpose(t, 1, X)
                wait(pe, otlo_done, 2, t, 1)
                project_out(t, 0, Z)
                wait(pe, otlo_done, 2, t, 2)
                project_out(t, 1, X)
                last_gates_of_state((0, 1, 2))
                wait(pe, gate_done, 6, t - 1, 5)
                x1_transpose(t, 0, Y)
                wait(pe, y_done, 2, t, 1)
                x1_transpose(t, 1, Z)
                last_gates_of_state((3, 4))
                for k in range(4):
                    gate_product(t, k, None)

            pe.wait_ge(const_ready, 2)
            pe.wait_ge(w_lo, 1)
            project_qk(0, 0, Z)
            project_qk(0, 1, X)
            pe.wait_ge(posrow, 16 * 8)
            iteration(0)
            pe.wait_ge(w_lo, 6)
            pe.wait_ge(c0_lo, 2)
            iteration(1)
            with pe.Fori(2, B - 1) as t:
                iteration(t)
            iteration(B - 1)
            last_sequence()
            iteration(B + 1)

            def transpose2(t, rnd, i):
                pe.wait_ge(x1_in[i], 16 * rnd + 16)
                if isinstance(t, int) and t < 2:
                    pe.wait_ge(gate_done, 6 * (B - 1) + 2 * t + 2)
                else:
                    pe.wait_ge(t2lo, 2 * t - 2)
                for c in range(KC):
                    for n in range(NB):
                        ins = te.transpose(banks[2 * (i % 2) + c][:, WIN * n:WIN * (n + 1)], ring[i][:, n, 128 * c:128 * c + 128], ident[:, :])
                    ins.then_inc(t2_ready, 1)

            def output(t, rnd, i):
                if not isinstance(t, int) or 1 < t + 1 < B:
                    transpose2(t + 1, rnd + (i + 1) // 4, (i + 1) % 4)
                pe.wait_ge(t2lo, 2 * t + 2)
                if not isinstance(t, int) or t >= 2:
                    pe.wait_ge(h_done, 2 * t - 2)
                elif t == 1:
                    pe.wait_ge(cu_sum, 2)
                for a in range(2):
                    bank = banks[4 + 2 * (i % 2) + a]
                    for n in (2 * a, 2 * a + 1):
                        for c in range(KC):
                            for wa, wb in PASSES:
                                te.matmul(bank[:, E * (n % 2):E * (n % 2) + E], parts2[i % 2][:, wa, c, n * WIN:(n + 1) * WIN],
                                          Wo[:, wb, c, :], start=(n % 2 == 0 and c == 0 and (wa, wb) == PASSES[0]),
                                          stop=False, skip_group_check=True)
                    if isinstance(t, int) and t == 0:
                        pe.wait_ge(culo_done, a + 1)
                    for part in range(2):
                        ins = te.matmul(bank[:, :], ident_r[:, :], cu[:, part, 2 * a:2 * a + 2, :].rearrange("p n e -> p (n e)"),
                                        start=False, stop=(part == 1), skip_group_check=True)
                    ins.then_inc(o2_ready, 1)

            transpose2(0, 0, 0)
            transpose2(1, 0, 1)
            pe.wait_ge(clo_done, 2 * B)
            for n in range(NB):
                product(banks[6 + n // 2][:, E * (n % 2):E * (n % 2) + E],
                        [(lambda a, c=c: cT[:, a, c, n * WIN:(n + 1) * WIN], lambda b, c=c: Uo[:, b, c, :])
                         for c in range(KC)], cu_ready if n % 2 else None)
            steps(pe, output)


def kernel(L0_attn_x, L0_attn_w_in, L0_attn_w_out, L0_ffn_wf, L0_ffn_uf, L0_ffn_bf, L0_ffn_wi, L0_ffn_ui, L0_ffn_bi,
           L0_ffn_wc, L0_ffn_uc, L0_ffn_bc, L0_ffn_wo, L0_ffn_uo, L0_ffn_bo, L0_ffn_in_c):
    import concourse.bacc as bacc
    from concourse.bass_utils import run_bass_kernel_spmd

    def rows(a):
        return np.ascontiguousarray(a)

    slopes = np.exp2(-(np.arange(H, dtype=np.float32) + 1.0) * 8.0 / H).astype(np.float32)
    positions = np.arange(S, dtype=np.float32) - S // 2
    tile = np.arange(S) // 32
    behind = (tile[None, :] - np.arange(N_TILES)[:, None]) % N_TILES
    left_out = np.where(behind > 4, np.float32(MASKED), np.float32(0))
    in_tile = (tile[None, :] % N_TILES == np.arange(N_TILES)[:, None]).astype(np.float32)
    tile_rows = np.ascontiguousarray(np.stack([left_out, in_tile], axis=1).astype(np.float32))
    arrays = {
        "x": rows(L0_attn_x),
        "xt": rows(np.transpose(L0_attn_x, (0, 2, 1))),
        "w_in": rows(np.transpose(L0_attn_w_in)),
        "w_out": rows(np.transpose(L0_attn_w_out)),
        "w_gates": rows(np.concatenate([np.transpose(w) for w in (L0_ffn_wf, L0_ffn_wi, L0_ffn_wc)], axis=1)),
        "u_gates": rows(np.concatenate([np.transpose(w) for w in (L0_ffn_uf, L0_ffn_ui, L0_ffn_uc)], axis=1)),
        "b_gates": rows(np.transpose(np.reshape(np.stack([L0_ffn_bf, L0_ffn_bi, L0_ffn_bc]), (3, KC, 128)), (2, 0, 1))),
        "w_o": rows(np.transpose(L0_ffn_wo)),
        "u_o": rows(np.transpose(L0_ffn_uo)),
        "b_o": rows(np.broadcast_to(np.reshape(L0_ffn_bo, (1, E)), (128, E))),
        "in_c": rows(np.transpose(np.reshape(L0_ffn_in_c, (KC, 128)))),
        "pos_bias": -np.concatenate([slopes[0::2], slopes[1::2]])[:, None] * positions[None, :],
        "tile_rows": tile_rows,
    }
    nc = bacc.Bacc("TRN2", target_bir_lowering=False, num_devices=1)
    args = [nc.dram_tensor(f"in_{n}", a.shape, mybir.dt.from_np(a.dtype), kind="ExternalInput").ap() for n, a in arrays.items()]
    result = nc.dram_tensor("result", (B, S, E), mybir.dt.float32, kind="ExternalOutput").ap()
    build(nc, *args, result)
    r = run_bass_kernel_spmd(nc, [{f"in_{n}": a for n, a in arrays.items()}], core_ids=[0])
    return r.results[0]["result"]
```
